# Optimizing a Trainium2 kernel written in Bass

```python
import numpy as np
import jax
import jax.numpy as jnp

def _softmax(x, axis=-1):
    return jax.nn.softmax(x, axis=axis)

def _gelu(x):
    return jax.nn.gelu(x, approximate=True)

def _silu(x):
    return jax.nn.silu(x)

def _sigmoid(x):
    return jax.nn.sigmoid(x)

def _layernorm(x, axis=-1, eps=1e-05):
    m = jnp.mean(x, axis=axis, keepdims=True)
    v = jnp.var(x, axis=axis, keepdims=True)
    return (x - m) / jnp.sqrt(v + eps)

def _scatter_add(tgt, idx, src, axis=0):
    return tgt.at[idx].add(src)

def _segment_sum(src, seg, n):
    return jax.ops.segment_sum(src, seg, n)
kernel_name = 'mk_gnn_resnorm_d4_gnn_r8_bbfccd'

def setup_inputs(seed: int=0):
    np.random.seed(seed)
    _w = jnp.asarray

    def _rec_inputs():
        import jax
        import jax.numpy as jnp
        _gk = jax.random.key(seed)
        x = -0.000202 + 1 * jax.random.normal(jax.random.fold_in(_gk, 1), (12500, 64), jnp.float32)
        _s = jax.random.randint(jax.random.fold_in(_gk, 2), (100000,), 0, 12500, jnp.int32)
        _d = jax.random.randint(jax.random.fold_in(_gk, 3), (100000,), 0, 12500, jnp.int32)
        _loop = jnp.arange(12500, dtype=jnp.int32)
        src = jnp.concatenate([_s, _d, _loop])
        dst = jnp.concatenate([_d, _s, _loop])
        _o = jnp.argsort(dst, stable=True)
        src = src[_o]
        dst = dst[_o]
        edge_attr_64 = 7.68618e-05 + 1.00005 * jax.random.normal(jax.random.fold_in(_gk, 13), (212500, 64), jnp.float32)
        edge_weight1 = jax.random.uniform(jax.random.fold_in(_gk, 15), (212500, 1), jnp.float32, 0.0, 1)
        return (x, src, dst, edge_attr_64, edge_weight1)
    x, src, dst, edge_attr_64, edge_weight1 = _rec_inputs()

    def _L0_gnn_setup():
        import jax, jax.numpy as jnp
        import numpy as np
        N = 12500
        E = 400000
        H = 64

        def _sage_conv(x, src, dst, Wl, bl, Wr, n_nodes):
            msgs = x[src]
            agg = jax.ops.segment_sum(msgs, dst, num_segments=n_nodes)
            deg = jax.ops.segment_sum(jnp.ones(src.shape[0], x.dtype), dst, num_segments=n_nodes)
            mean = agg / jnp.maximum(deg, 1.0)[:, None]
            return mean @ Wl.T + bl + x @ Wr.T
        key = jax.random.key(seed)
        ks = jax.random.split(key, 12)
        s = 1.0 / np.sqrt(H)
        u = lambda k, shp: jax.random.uniform(k, shp, jnp.float32, -s, s)
        x = jax.random.normal(ks[0], (N, H), jnp.float32)
        edge_index = jax.random.randint(ks[1], (2, E), 0, N, jnp.int32)
        return {'x': x, 'edge_index': edge_index, 'conv1_Wl': u(ks[2], (H, H)), 'conv1_bl': u(ks[3], (H,)), 'conv1_Wr': u(ks[4], (H, H)), 'mlp_W1': u(ks[5], (H, H)), 'mlp_b1': u(ks[6], (H,)), 'mlp_W2': u(ks[7], (H, H)), 'mlp_b2': u(ks[8], (H,)), 'conv2_Wl': u(ks[9], (H, H)), 'conv2_bl': u(ks[10], (H,)), 'conv2_Wr': u(ks[11], (H, H))}
    _L0_gnn_all = _L0_gnn_setup()
    _L0_gnn_in = {k: v for k, v in _L0_gnn_all.items() if k in ('conv1_Wl', 'conv1_bl', 'conv1_Wr', 'mlp_W1', 'mlp_b1', 'mlp_W2', 'mlp_b2', 'conv2_Wl', 'conv2_bl', 'conv2_Wr')}
    del _L0_gnn_all

    def _L1_gnn_setup():
        import jax, jax.numpy as jnp
        import numpy as np
        EPS = 1e-05

        def _mlp(h, W, b, gamma, beta):
            h = h @ W + b
            mu = jnp.mean(h, axis=0)
            var = jnp.var(h, axis=0)
            h = (h - mu) * jax.lax.rsqrt(var + EPS) * gamma + beta
            return h * jax.nn.sigmoid(h)
        key = jax.random.key(seed)
        ks = jax.random.split(key, 10)
        N, E, D, G = (12500, 125000, 64, 16)
        x = jax.random.normal(ks[0], (N, D), dtype=jnp.float32)
        edge_index = jax.random.randint(ks[1], (2, E), 0, N, dtype=jnp.int64)
        edge_attr = jax.random.normal(ks[2], (E, D), dtype=jnp.float32)
        u = jax.random.normal(ks[3], (G, D), dtype=jnp.float32)
        batch = jax.random.randint(ks[4], (N,), 0, G, dtype=jnp.int64)
        s1 = 1.0 / np.sqrt(2 * D)
        W1 = jax.random.uniform(ks[5], (2 * D, D), jnp.float32, -s1, s1)
        b1 = jax.random.uniform(ks[6], (D,), jnp.float32, -s1, s1)
        W2 = jax.random.uniform(ks[7], (2 * D, D), jnp.float32, -s1, s1)
        b2 = jax.random.uniform(ks[8], (D,), jnp.float32, -s1, s1)
        g1 = jnp.ones((D,), jnp.float32)
        be1 = jnp.zeros((D,), jnp.float32)
        g2 = jnp.ones((D,), jnp.float32)
        be2 = jnp.zeros((D,), jnp.float32)
        return {'x': x, 'edge_attr': edge_attr, 'u': u, 'W1': W1, 'b1': b1, 'g1': g1, 'be1': be1, 'W2': W2, 'b2': b2, 'g2': g2, 'be2': be2, 'edge_index': edge_index, 'batch': batch}
    _L1_gnn_all = _L1_gnn_setup()
    _L1_gnn_in = {k: v for k, v in _L1_gnn_all.items() if k in ('u', 'W1', 'b1', 'g1', 'be1', 'W2', 'b2', 'g2', 'be2')}
    del _L1_gnn_all

    def _L2_gnn_setup():
        import jax, jax.numpy as jnp
        import numpy as np
        N_NODES = 12500
        N_EDGES = 200000
        IN_FEAT = 64
        OUT_FEAT = 64
        key = jax.random.key(seed)
        k1, k2, k3, k4, k5 = jax.random.split(key, 5)
        feat = jax.random.normal(k1, (N_NODES, IN_FEAT), dtype=jnp.float32)
        attention = jax.random.uniform(k2, (N_EDGES, 1), dtype=jnp.float32)
        src = jax.random.randint(k3, (N_EDGES,), 0, N_NODES, dtype=jnp.int32)
        dst = jax.random.randint(k4, (N_EDGES,), 0, N_NODES, dtype=jnp.int32)
        gain = float(np.sqrt(2.0))
        limit = gain * np.sqrt(6.0 / (IN_FEAT + OUT_FEAT))
        weight = jax.random.uniform(k5, (IN_FEAT, OUT_FEAT), dtype=jnp.float32, minval=-limit, maxval=limit)
        h_bias = jnp.zeros((OUT_FEAT,), dtype=jnp.float32)
        return {'feat': feat, 'attention': attention, 'src': src, 'dst': dst, 'weight': weight, 'h_bias': h_bias}
    _L2_gnn_all = _L2_gnn_setup()
    _L2_gnn_in = {k: v for k, v in _L2_gnn_all.items() if k in ('weight', 'h_bias')}
    del _L2_gnn_all

    def _L3_gnn_setup():
        import jax, jax.numpy as jnp
        import numpy as np
        N = 12500
        E = 150000
        IN_DIM = 64
        OUT_DIM = 64
        K = 3
        key = jax.random.key(seed)
        k1, k2, k3 = jax.random.split(key, 3)
        x = jax.random.normal(k1, (N, IN_DIM), dtype=jnp.float32)
        edge_index = jax.random.randint(k2, (2, E), 0, N, dtype=jnp.int64)
        W = jax.random.normal(k3, (IN_DIM, OUT_DIM), dtype=jnp.float32) * (1.0 / np.sqrt(IN_DIM))
        b = jnp.zeros((OUT_DIM,), dtype=jnp.float32)
        return {'x': x, 'edge_index': edge_index, 'W': W, 'b': b}
    _L3_gnn_all = _L3_gnn_setup()
    _L3_gnn_in = {k: v for k, v in _L3_gnn_all.items() if k in ('W', 'b')}
    del _L3_gnn_all
    return {'x': x, 'src': src, 'dst': dst, 'edge_attr_64': edge_attr_64, 'edge_weight1': edge_weight1, 'L0_gnn_conv1_Wl': _L0_gnn_in['conv1_Wl'], 'L0_gnn_conv1_bl': _L0_gnn_in['conv1_bl'], 'L0_gnn_conv1_Wr': _L0_gnn_in['conv1_Wr'], 'L0_gnn_mlp_W1': _L0_gnn_in['mlp_W1'], 'L0_gnn_mlp_b1': _L0_gnn_in['mlp_b1'], 'L0_gnn_mlp_W2': _L0_gnn_in['mlp_W2'], 'L0_gnn_mlp_b2': _L0_gnn_in['mlp_b2'], 'L0_gnn_conv2_Wl': _L0_gnn_in['conv2_Wl'], 'L0_gnn_conv2_bl': _L0_gnn_in['conv2_bl'], 'L0_gnn_conv2_Wr': _L0_gnn_in['conv2_Wr'], 'L1_gnn_u': _L1_gnn_in['u'], 'L1_gnn_W1': _L1_gnn_in['W1'], 'L1_gnn_b1': _L1_gnn_in['b1'], 'L1_gnn_g1': _L1_gnn_in['g1'], 'L1_gnn_be1': _L1_gnn_in['be1'], 'L1_gnn_W2': _L1_gnn_in['W2'], 'L1_gnn_b2': _L1_gnn_in['b2'], 'L1_gnn_g2': _L1_gnn_in['g2'], 'L1_gnn_be2': _L1_gnn_in['be2'], 'L2_gnn_weight': _L2_gnn_in['weight'], 'L2_gnn_h_bias': _L2_gnn_in['h_bias'], 'L3_gnn_W': _L3_gnn_in['W'], 'L3_gnn_b': _L3_gnn_in['b']}

def reference(x, src, dst, edge_attr_64, edge_weight1, L0_gnn_conv1_Wl, L0_gnn_conv1_bl, L0_gnn_conv1_Wr, L0_gnn_mlp_W1, L0_gnn_mlp_b1, L0_gnn_mlp_W2, L0_gnn_mlp_b2, L0_gnn_conv2_Wl, L0_gnn_conv2_bl, L0_gnn_conv2_Wr, L1_gnn_u, L1_gnn_W1, L1_gnn_b1, L1_gnn_g1, L1_gnn_be1, L1_gnn_W2, L1_gnn_b2, L1_gnn_g2, L1_gnn_be2, L2_gnn_weight, L2_gnn_h_bias, L3_gnn_W, L3_gnn_b):
    import jax
    import jax.numpy as jnp

    def _L0_gnn_ref(x, edge_index, conv1_Wl, conv1_bl, conv1_Wr, mlp_W1, mlp_b1, mlp_W2, mlp_b2, conv2_Wl, conv2_bl, conv2_Wr):
        import jax, jax.numpy as jnp
        import numpy as np
        N = 12500
        E = 400000
        H = 64

        def _sage_conv(x, src, dst, Wl, bl, Wr, n_nodes):
            msgs = x[src]
            agg = jax.ops.segment_sum(msgs, dst, num_segments=n_nodes)
            deg = jax.ops.segment_sum(jnp.ones(src.shape[0], x.dtype), dst, num_segments=n_nodes)
            mean = agg / jnp.maximum(deg, 1.0)[:, None]
            return mean @ Wl.T + bl + x @ Wr.T
        src, dst = (edge_index[0], edge_index[1])
        n = x.shape[0]
        h = jax.nn.relu(_sage_conv(x, src, dst, conv1_Wl, conv1_bl, conv1_Wr, n))
        h = jax.nn.relu(h @ mlp_W1.T + mlp_b1) @ mlp_W2.T + mlp_b2
        out = _sage_conv(h, src, dst, conv2_Wl, conv2_bl, conv2_Wr, n)
        return out

    def _L1_gnn_ref(x, edge_attr, u, W1, b1, g1, be1, W2, b2, g2, be2, edge_index, batch):
        import jax, jax.numpy as jnp
        import numpy as np
        EPS = 1e-05

        def _mlp(h, W, b, gamma, beta):
            h = h @ W + b
            mu = jnp.mean(h, axis=0)
            var = jnp.var(h, axis=0)
            h = (h - mu) * jax.lax.rsqrt(var + EPS) * gamma + beta
            return h * jax.nn.sigmoid(h)
        N = x.shape[0]
        row, col = (edge_index[0], edge_index[1])
        msg = _mlp(jnp.concatenate([x[row], edge_attr], axis=1), W1, b1, g1, be1)
        sums = jax.ops.segment_sum(msg, col, num_segments=N)
        cnt = jax.ops.segment_sum(jnp.ones((msg.shape[0],), msg.dtype), col, num_segments=N)
        agg = sums / jnp.maximum(cnt, 1.0)[:, None]
        return _mlp(jnp.concatenate([x, agg], axis=1), W2, b2, g2, be2)

    def _L2_gnn_ref(feat, attention, src, dst, weight, h_bias):
        import jax, jax.numpy as jnp
        import numpy as np
        N_NODES = 12500
        N_EDGES = 200000
        IN_FEAT = 64
        OUT_FEAT = 64
        h = feat @ weight + h_bias
        m = h[src] * attention
        out = jax.ops.segment_sum(m, dst, num_segments=feat.shape[0])
        return out

    def _L3_gnn_ref(x, edge_index, W, b):
        import jax, jax.numpy as jnp
        import numpy as np
        N = 12500
        E = 150000
        IN_DIM = 64
        OUT_DIM = 64
        K = 3
        n = x.shape[0]
        src = edge_index[0]
        dst = edge_index[1]
        loop = jnp.arange(n, dtype=src.dtype)
        src = jnp.concatenate([src, loop])
        dst = jnp.concatenate([dst, loop])
        deg = jax.ops.segment_sum(jnp.ones(src.shape[0], dtype=x.dtype), dst, num_segments=n)
        dinv = jnp.where(deg > 0, jax.lax.rsqrt(jnp.where(deg > 0, deg, 1.0)), 0.0)
        norm = dinv[src] * dinv[dst]
        h = x
        for _ in range(K):
            h = jax.ops.segment_sum(norm[:, None] * h[src], dst, num_segments=n)
        return h @ W + b
    edge_index = jnp.stack([src, dst])
    batch0 = jnp.zeros((12500,), jnp.int32)
    x = _layernorm(x + _L0_gnn_ref(x, edge_index, L0_gnn_conv1_Wl, L0_gnn_conv1_bl, L0_gnn_conv1_Wr, L0_gnn_mlp_W1, L0_gnn_mlp_b1, L0_gnn_mlp_W2, L0_gnn_mlp_b2, L0_gnn_conv2_Wl, L0_gnn_conv2_bl, L0_gnn_conv2_Wr), axis=-1)
    x = _layernorm(x + _L1_gnn_ref(x, edge_attr_64, L1_gnn_u, L1_gnn_W1, L1_gnn_b1, L1_gnn_g1, L1_gnn_be1, L1_gnn_W2, L1_gnn_b2, L1_gnn_g2, L1_gnn_be2, edge_index, batch0), axis=-1)
    x = _layernorm(x + _L2_gnn_ref(x, edge_weight1, src, dst, L2_gnn_weight, L2_gnn_h_bias), axis=-1)
    x = _layernorm(x + _L3_gnn_ref(x, edge_index, L3_gnn_W, L3_gnn_b), axis=-1)
    return x

_drawn_inputs = setup_inputs


def setup_inputs(seed=0):
    import zlib

    import numpy as np

    out = dict(_drawn_inputs(seed))
    spreads = {'L1_gnn_g1': (1.0, 0.6),
     'L1_gnn_be1': (0.0, 0.8),
     'L1_gnn_g2': (1.0, 0.2),
     'L1_gnn_be2': (0.0, 0.1),
     'L2_gnn_h_bias': (0.0, 0.1),
     'L3_gnn_b': (0.0, 0.1)}
    factors = {'L0_gnn_conv1_Wl': 4.171, 'L0_gnn_conv1_bl': 2.69, 'L1_gnn_b1': 8.0, 'L1_gnn_b2': 8.0}
    for name, (base, spread) in spreads.items():
        noise = np.random.default_rng([zlib.crc32(name.encode()), seed]).standard_normal(out[name].shape)
        drawn = base * np.exp(spread * noise) if base else spread * noise
        out[name] = jnp.asarray(drawn.astype(out[name].dtype))
    for name, factor in factors.items():
        out[name] = (out[name] * factor).astype(out[name].dtype)
    return out
```

```python
import concourse.bass as bass
from concourse import mybir
from contextlib import ExitStack

P = 128
N = 12500
E = 212500
H = 64
NT = -(-N // P)
NP = NT * P
C = 13
GROUPS = -(-E // (P * C))
ITERS = GROUPS // 2
CA = (C + 1) // 2
CB = C - CA
W = 128
TB = 7
NB = NT // TB
BN = TB * P
HB = BN // 2
DITERS = NB // 2
EPS = 1e-5
assert GROUPS == P and NB * TB == NT and NB % 2 == 0

W_CONV1, W_MLP1, W_MLP2, W_CONV2, W_L1X, W_L1E, W_L1Z, W_L2, W_L3 = 0, 1, 2, 4, 5, 6, 7, 8, 9
C_BL1, C_B1, C_B2, C_BZ, C_G2, C_BE2 = range(6)
R_B2, R_BL2, R_B1, R_HB, R_B3, R_G1, R_BE1 = range(7)


def gnn_program(nc, x_rows, x_feat, src_idx, dst_idx, att, edge_feat, consts, valid, weights, cols, rows, out):
    f32, i32 = mybir.dt.float32, mybir.dt.int32
    ALU, ACT, AX = mybir.AluOpType, mybir.ActivationFunctionType, mybir.AxisListType
    V, S, T = nc.vector, nc.scalar, nc.tensor
    ctx = ExitStack()
    with ctx:
        def sb(name, shape, dt=f32):
            return ctx.enter_context(nc.sbuf_tensor(name, shape, dt))

        def sem(name):
            return ctx.enter_context(nc.semaphore(name))

        def sems(name, n=2):
            return [sem(f"{name}{i}") for i in range(n)]

        def dram(name, shape):
            return nc.dram_tensor(name, shape, f32, kind="Internal").ap()

        tab_h2, tab_l1, tab_l2 = dram("tab_h2", [NP, H]), dram("tab_l1", [NP, H]), dram("tab_l2", [NP, H])
        tab_hop = [dram(f"tab_hop{k}", [NP, H]) for k in range(3)]
        edge_h = dram("edge_h", [GROUPS, P, C * H])

        feat = sb("feat", [P, NP + W])
        wide = sb("wide", [P, NP])
        rdeg = wide[0:H, :]
        resid = sb("resid", [P, NT, H])
        hop = wide[:, 0:NT * H].rearrange("p (t f) -> p t f", f=H)
        dst_f = sb("dst_f", [P, GROUPS, C])
        att_s = sb("att_s", [P, GROUPS, C])
        idx = sb("idx", [P, 2, C], i32)
        gath = sb("gath", [P, 2, C, 2 * H])
        oneh = sb("oneh", [P, 2, C, W])
        accum = sb("accum", [P, 2, C, H])
        cst = sb("cst", [P, 2, P])
        ident, iota0 = cst[:, 0, :], cst[:, 1, :]
        val = sb("val", [P, NT])
        iota_w = sb("iota_w", [P, 1, W])
        ones = sb("ones", [P, P])
        wts = sb("wts", [P, weights.shape[1], H])
        col = sb("col", [P, cols.shape[1]])
        row = sb("row", [P, rows.shape[1], H])
        lim = sb("lim", [P, 4])
        diag = sb("diag", [P, P])
        base_f = sb("base_f", [P, GROUPS])
        base_i = sb("base_i", [1, GROUPS], i32)
        base_w = sb("base_w", [1, GROUPS], i32)
        span_i = sb("span_i", [1, 1], i32)
        deg_n = sb("deg_n", [P, NT])
        dinv = sb("dinv", [P, NT])
        dinv2 = sb("dinv2", [P, NT])
        bn = sb("bn", [P, 4, H])
        bnz = sb("bnz", [H, 4])
        stats = sb("stats", [H, 2 * NB, 6])
        sta = sb("sta", [P, 2, BN])
        stb = sb("stb", [P, 2, BN])
        nod = sb("nod", [P, 2, 3, TB, H])
        ln = sb("ln", [P, 2, 3, TB])
        eft = sta
        ebuf = stb[:, :, 0:C * H].rearrange("p s (c f) -> p s c f", f=H)
        emsg = nod[:, :, :, :, :].rearrange("p s a t f -> p s (a t f)")[:, :, 0:C * H]\
            .rearrange("p s (c f) -> p s c f", f=H)
        eps = sb("eps", [P, 1])

        bank = [ctx.enter_context(nc.psum_tensor(f"bank{i}", [P, 512], f32)) for i in range(8)]

        s_dst, s_par, s_att, s_xf, s_deg = sem("dst_in"), sem("params_in"), sem("att_in"), sem("xfeat_in"), sem("deg_moved")
        s_set = sem("constants_set")
        s_lim = sem("setup_steps")
        s_win = sem("windows_known")
        s_gate = sem("gate")
        s_pre = sem("pass_prepared")
        s_shift = sem("windows_shifted")
        s_pass = sem("pass_done")
        s_table = sem("table_stored")
        s_weighed = sem("onehots_placed")

        def hold(eng, s, value):
            eng.wait_ge(s, value)
            eng.sem_inc(s_gate, 1)

        class Pass:

            def __init__(self, name):
                self.idx_in = sems(f"{name}_idx_in")
                self.rows_in = sems(f"{name}_rows_in")
                self.onehot = sem(f"{name}_onehot")
                self.summed = sem(f"{name}_summed")
                self.added = sem(f"{name}_added")

        p_conv1, p_conv2, p_edge, p_msg, p_att = (Pass(n) for n in ("conv1", "conv2", "edge", "msg", "att"))
        p_hop = [Pass(f"hop{k}") for k in range(3)]
        s_ef = sems("edge_feat_in")
        s_emm = sem("edge_product")
        s_eh = sem("edge_act")
        s_esq = sem("edge_squared")
        s_eacc = sems("edge_accumulated")
        s_est = sems("edge_stored")
        s_hl, s_mul = sems("act_loaded"), sem("act_scaled")
        s_mad, s_msg = sem("act_shifted"), sem("message")
        s_bn, s_bnz, s_dg = sem("bn_steps"), sem("bnz_steps"), sem("degree_steps")

        class Turns:

            def __init__(self, name, steps):
                self.turn, self.stored, self.steps = sems(f"{name}_turn"), sems(f"{name}_stored"), steps

            def wait(self, eng, i, h, step):
                hold(eng, self.turn[h], i * self.steps + step)

        def done(ins, d, h):
            ins.then_inc(d.turn[h], 1)

        d_conv1, d_conv2, d_z, d_l1, d_l2 = (Turns("d_conv1", 12), Turns("d_conv2", 20), Turns("d_z", 4),
                                             Turns("d_l1", 16), Turns("d_l2", 14))
        d_hop = [Turns("d_hop0", 5), Turns("d_hop1", 5), Turns("d_hop2", 17)]

        block = ctx.enter_context(nc.Block())

        def n_windows(eng):
            eng.wait_ge(s_win, 1)
            return eng.value_load(span_i[0:1, 0:1], min_val=0, max_val=NP) // W + 1

        def group(t, g):
            return t[bass.ds(g, 1), :, :].rearrange("a p c -> (a p) c")

        def load_lists(sp, p, n_win, used, edge=False):
            with sp.Fori(0, n_win) as w:
                with sp.Fori(0, ITERS) as i:
                    for h in range(2):
                        hold(sp, used, 2 * (w * ITERS + i) + h + 1)
                        sp.dma_start(idx[:, h, :], group(src_idx, 2 * i + h)).then_inc(p.idx_in[h], 16)
                        if edge:
                            sp.dma_start(eft[:, h, :], group(edge_feat, 2 * i + h)).then_inc(s_ef[h], 16)

        def gather(pool, p, n_win, table):
            with pool.Fori(0, n_win) as w:
                with pool.Fori(0, ITERS) as i:
                    for h in range(2):
                        hold(pool, p.idx_in[h], 16 * (w * ITERS + i + 1))
                        for c in range(C):
                            pool.indirect_dma_start(
                                out=gath[:, h, c, 0:H], out_offset=None, in_=table[:, :],
                                in_offset=bass.IndirectOffsetOnAxis(ap=idx[:, h, c:c + 1], axis=0),
                            ).then_inc(p.rows_in[h], 16)

        def sum_groups(pe, p, n_win, rows_of, rows_are_in, width=H):
            pe.sem_inc(p.summed, 2)
            with pe.Fori(0, n_win) as w:
                with pe.Fori(0, ITERS) as i:
                    for h in range(2):
                        q = 2 * (w * ITERS + i) + h
                        rows_are_in(pe, w * ITERS + i, h)
                        hold(pe, p.onehot, q + 1)
                        hold(pe, p.added, q + 1)
                        for c in range(C):
                            last = T.matmul(bank[h][0:width, 0:W], rows_of(h, c), oneh[:, h, c, :],
                                            start=(c == 0), stop=(c == C - 1))
                        last.then_inc(p.summed, 1)

        def gathered(p):
            return lambda pe, k, h: hold(pe, p.rows_in[h], 16 * C * (k + 1))

        passes = [0]

        def add_windows(dve, p, n_win, width=H, weigh=False, scale=None):
            V.memset(feat[0:width, :], 0.0).then_inc(s_pre, 1)
            V.tensor_copy(iota_w[:, 0, :], iota0).then_inc(s_pre, 1)
            V.tensor_copy(base_w[:, :], base_i[:, :]).then_inc(s_pre, 1)
            before = passes[0]
            passes[0] += 1
            dve.wait_ge(s_pre, 3 * passes[0])
            dve.sem_inc(p.added, 2)
            with dve.Fori(0, n_win) as w:
                with dve.Fori(0, ITERS) as i:
                    for h in range(2):
                        q = 2 * (w * ITERS + i) + h
                        if scale is not None:
                            scale(dve, w * ITERS + i, h)
                        hold(dve, p.summed, q + 1)
                        ins = V.tensor_tensor(
                            oneh[:, h, :, :], iota_w[:, :, :].to_broadcast([P, C, W]),
                            dst_f[:, bass.ds(2 * i + h, 1), :].rearrange("p a (c o) -> p (a c) o", o=1)
                            .to_broadcast([P, C, W]), ALU.is_equal)
                        if weigh:
                            ins.then_inc(s_weighed, 1)
                            hold(dve, s_weighed, q + 1)
                            ins = V.tensor_tensor(
                                oneh[:, h, :, :], oneh[:, h, :, :],
                                att_s[:, bass.ds(2 * i + h, 1), :].rearrange("p a (c o) -> p (a c) o", o=1)
                                .to_broadcast([P, C, W]), ALU.mult)
                        ins.then_inc(p.onehot, 1)
                    for h in range(2):
                        q = 2 * (w * ITERS + i) + h
                        first = dve.value_load(base_w[0:1, bass.ds(2 * i + h, 1)], min_val=0, max_val=NP)
                        hold(dve, p.summed, q + 3)
                        hold(dve, p.added, q + 2)
                        V.tensor_tensor(feat[0:width, bass.ds(first, W)], feat[0:width, bass.ds(first, W)],
                                        bank[h][0:width, 0:W], ALU.add).then_inc(p.added, 1)
                hold(dve, p.added, 2 * ITERS * (w + 1) + 2)
                V.tensor_scalar(iota_w[:, 0, :], iota_w[:, 0, :], float(W), None, ALU.add).then_inc(s_shift, 1)
                V.tensor_scalar(base_w[:, :], base_w[:, :], float(W), float(NP), ALU.add, ALU.min)\
                    .then_inc(s_shift, 1)
                hold(dve, s_shift, 2 * (n_win * before + w + 1))
            dve.sem_inc(s_pass, 1)

        def blk(t, lo, hi, b, half=None):
            if half is None:
                return t[lo:hi, bass.ds(b * BN, BN)]
            return t[lo:hi, bass.ds(b * BN + half * HB, HB)]

        def tiles(t, b):
            return t[:, bass.ds(b * TB, TB), :]

        def by_tile(t, b):
            return t[:, bass.ds(b * TB, TB)].rearrange("p (t o) -> p t o", o=1).to_broadcast([P, TB, H])

        def over_features(t):
            return t.rearrange("p (t o) -> p t o", o=1).to_broadcast([P, TB, H])

        def row_b(r):
            return row[:, r:r + 1, :].to_broadcast([P, TB, H])

        def nb(h, j):
            return bank[4 * h + j]

        def nodes(h, j):
            return nb(h, j)[:, 0:TB * H].rearrange("p (t f) -> p t f", t=TB)

        def halves(t, h, lo, hi):
            return [t[lo:hi, h, j * HB:(j + 1) * HB] for j in range(2)]

        def turns(eng, d, steps):
            with eng.Fori(0, DITERS) as i:
                for step, work in steps:
                    for h in range(2):
                        d.wait(eng, i, h, step)
                        done(work(2 * i + h, h), d, h)

        def open_turns(pe, d):
            for h in range(2):
                pe.sem_inc(d.turn[h], 1)

        def store(sp, d, table):
            for h in range(2):
                sp.sem_inc(d.stored[h], 16)
            with sp.Fori(0, DITERS) as i:
                for h in range(2):
                    hold(sp, d.turn[h], (i + 1) * d.steps + 1)
                    sp.dma_start(table[bass.ds((2 * i + h) * BN, BN), :].rearrange("(t p) f -> p t f", p=P),
                                 nod[:, h, 0, :, :]).then_inc(d.stored[h], 16)
            for h in range(2):
                sp.wait_ge(d.stored[h], 16 * DITERS + 16)
            sp.sem_inc(s_table, 1)

        def stored(eng, d, i_block, h):
            hold(eng, d.stored[h], 16 * ((i_block - h) // 2) + 16)

        def feat_by_node(b, h):
            for t in range(TB):
                last = T.matmul(nb(h, 0)[:, t * H:(t + 1) * H], sta[0:H, h, t * P:(t + 1) * P], ident[0:H, 0:H],
                                start=True, stop=True)
            return last

        def node_by_feat(src):
            def work(b, h):
                for t in range(TB):
                    j, at = divmod(t, 4)
                    last = T.matmul(nb(h, 1 + j)[H:P, at * P:(at + 1) * P], nod[:, h, src, t, :], ident,
                                    start=True, stop=True)
                return last
            return work

        def take_feat(b, h):
            S.copy(sta[H:P, h, 0:4 * P], nb(h, 1)[H:P, 0:4 * P])
            return S.copy(sta[H:P, h, 4 * P:BN], nb(h, 2)[H:P, 0:3 * P])

        def times_w(w):
            def work(b, h):
                for t in range(TB):
                    last = T.matmul(nb(h, 3)[:, t * H:(t + 1) * H], sta[H:P, h, t * P:(t + 1) * P], wts[H:P, w, :],
                                    start=True, stop=True)
                return last
            return work

        def sums_to_sta(b, h):
            return S.copy(sta[0:H, h, :], blk(feat, 0, H, b))

        def ln_sum(b, h):
            return V.tensor_reduce(ln[:, h, 0, :], nod[:, h, 1, :, :], AX.X, ALU.add)

        def ln_mean(b, h):
            return V.tensor_scalar(ln[:, h, 0, :], ln[:, h, 0, :], -1.0 / H, None, ALU.mult)

        def ln_center(b, h):
            return V.tensor_tensor(nod[:, h, 1, :, :], nod[:, h, 1, :, :], over_features(ln[:, h, 0, :]), ALU.add)

        def ln_square(b, h):
            return S.activation(nod[:, h, 2, :, :], nod[:, h, 1, :, :], ACT.Square)

        def ln_var(b, h):
            return V.tensor_reduce(ln[:, h, 1, :], nod[:, h, 2, :, :], AX.X, ALU.add)

        def ln_std(b, h):
            return S.activation(ln[:, h, 1, :], ln[:, h, 1, :], ACT.Sqrt, bias=eps[:, :], scale=1.0 / H)

        def ln_rstd(b, h):
            return V.reciprocal(ln[:, h, 1, :], ln[:, h, 1, :])

        def ln_scale(to):
            def work(b, h):
                return V.tensor_tensor(nod[:, h, to, :, :], nod[:, h, 1, :, :], over_features(ln[:, h, 1, :]),
                                       ALU.mult)
            return work

        def keep_resid(b, h):
            return S.copy(tiles(resid, b), nod[:, h, 1, :, :])

        def ln_dve(first):
            return [(first, ln_sum), (first + 1, ln_mean), (first + 2, ln_center), (first + 4, ln_var),
                    (first + 6, ln_rstd)]

        def ln_act(first):
            return [(first + 3, ln_square), (first + 5, ln_std)]

        def add_resid(b, h, j=0):
            return V.tensor_tensor(nod[:, h, 1, :, :], nodes(h, j), tiles(resid, b), ALU.add)

        @block.sync
        def _(sp):
            sp.dma_start(wide[:, 0:C * GROUPS].bitcast(i32), dst_idx)\
                .then_inc(s_dst, 16)
            sp.dma_start(cst[:, :, :], consts).then_inc(s_dst, 16)
            for t, src in ((wts[:, :, :], weights), (col[:, :], cols), (row[:, :, :], rows), (val[:, :], valid),
                           (resid[:, :, :], x_rows.rearrange("(t p) f -> p t f", p=P))):
                sp.dma_start(t, src).then_inc(s_par, 16)
            sp.dma_start(att_s[:, :, :], att).then_inc(s_att, 16)
            n_win = n_windows(sp)

            load_lists(sp, p_conv1, n_win, p_conv1.summed)
            sp.wait_ge(s_pass, 1)
            sp.dma_start(rdeg[:, :], feat[H:P, 0:NP]).then_inc(s_deg, 16)
            sp.wait_ge(s_deg, 16)
            sp.dma_start(feat[H:P, 0:NP], x_feat).then_inc(s_xf, 16)
            store(sp, d_conv1, tab_h2)
            load_lists(sp, p_conv2, n_win, p_conv2.summed)
            store(sp, d_conv2, tab_l1)

            load_lists(sp, p_edge, 1, s_eh, edge=True)
            for h in range(2):
                sp.wait_ge(s_est[h], 16 * ITERS + 16)
            sp.wait_ge(s_bn, 1)
            with sp.Fori(0, n_win) as w:
                with sp.Fori(0, ITERS) as i:
                    for h in range(2):
                        hold(sp, s_msg, 2 * (w * ITERS + i) + h + 1)
                        sp.dma_start(ebuf[:, h, :, :].rearrange("p c f -> p (c f)"),
                                     group(edge_h, 2 * i + h)).then_inc(s_hl[h], 16)
            store(sp, d_l1, tab_l2)
            load_lists(sp, p_att, n_win, p_att.summed)
            store(sp, d_l2, tab_hop[0])
            for k in range(3):
                load_lists(sp, p_hop[k], n_win, p_hop[k].summed)
                store(sp, d_hop[k], tab_hop[k + 1] if k < 2 else out)

        @block.gpsimd
        def _(pool):
            pool.memset(gath[:, :, :, :], 1.0).then_inc(s_set, 1)
            pool.memset(ones[:, :], 1.0).then_inc(s_set, 1)
            pool.memset(eps[:, :], EPS).then_inc(s_set, 1)
            pool.wait_ge(s_set, 3)
            n_win = n_windows(pool)
            gather(pool, p_conv1, n_win, x_rows)
            pool.wait_ge(s_table, 1)
            gather(pool, p_conv2, n_win, tab_h2)
            pool.wait_ge(s_table, 2)
            gather(pool, p_edge, 1, tab_l1)
            pool.wait_ge(s_bn, 10)
            with pool.Fori(0, n_win) as w:
                with pool.Fori(0, ITERS) as i:
                    for h in range(2):
                        hold(pool, s_hl[h], 16 * (w * ITERS + i + 1))
                        pool.tensor_tensor(ebuf[:, h, :, :], ebuf[:, h, :, :],
                                           bn[:, 1:2, :].to_broadcast([P, C, H]), ALU.mult).then_inc(s_mul, 1)
            pool.wait_ge(s_table, 3)
            gather(pool, p_att, n_win, tab_l2)
            for k in range(3):
                pool.wait_ge(s_table, 4 + k)
                gather(pool, p_hop[k], n_win, tab_hop[k])

        @block.scalar
        def _(act):
            act.wait_ge(s_par, 80)
            act.wait_ge(s_set, 3)

            def relu(to, j0, c):
                def work(b, h):
                    for j in range(2):
                        last = S.activation(halves(to, h, 0, H)[j], nb(h, j0 + j)[0:H, 0:HB], ACT.Relu,
                                            bias=col[0:H, c:c + 1])
                    return last
                return work

            def h_to_root(b, h):
                for j in range(2):
                    last = S.activation(blk(feat, H, P, b, j), nb(h, j)[H:P, 0:HB], ACT.Identity,
                                        bias=col[H:P, C_B2:C_B2 + 1])
                return last

            turns(act, d_conv1, [(7, relu(sta, 0, C_BL1)), (9, relu(stb, 2, C_B1)), (11, h_to_root)])
            act.wait_ge(s_dg, 2)
            S.activation(dinv[:, :], dinv2[:, :], ACT.Sqrt).then_inc(s_dg, 1)

            def root_to_sta(b, h):
                return S.copy(sta[H:P, h, :], blk(feat, H, P, b))

            def sta_to_root(b, h):
                return S.copy(blk(feat, H, P, b), sta[H:P, h, :])

            turns(act, d_conv2, [(2, root_to_sta), *ln_act(6), (14, keep_resid), (16, take_feat), (17, sta_to_root)])

            for h in range(2):
                act.sem_inc(s_est[h], 16)
            with act.Fori(0, ITERS) as i:
                for h in range(2):
                    hold(act, s_eh, 2 * i + h + 3)
                    hold(act, s_eacc[1], 2 * i + h + 1)
                    S.activation(emsg[:, h, :, :], ebuf[:, h, :, :], ACT.Square).then_inc(s_esq, 1)
                    act.dma_start(group(edge_h, 2 * i + h), ebuf[:, h, :, :].rearrange("p c f -> p (c f)"))\
                        .then_inc(s_est[h], 16)
            act.wait_ge(s_bn, 5)
            S.activation(bn[:, 2, :], bn[:, 1, :], ACT.Sqrt, bias=eps[:, :]).then_inc(s_bn, 1)
            act.sem_inc(s_msg, 2)
            n_win = n_windows(act)
            with act.Fori(0, n_win) as w:
                with act.Fori(0, ITERS) as i:
                    for h in range(2):
                        q = 2 * (w * ITERS + i) + h
                        hold(act, s_mad, q + 1)
                        hold(act, p_msg.summed, q + 1)
                        S.activation(emsg[:, h, :, :], ebuf[:, h, :, :], ACT.Silu).then_inc(s_msg, 1)

            def z_to_feat(b, h):
                for j in range(2):
                    last = S.activation(blk(feat, 0, H, b, j), nb(h, j)[0:H, 0:HB], ACT.Identity,
                                        bias=col[0:H, C_BZ:C_BZ + 1])
                return last

            turns(act, d_z, [(3, z_to_feat)])
            act.wait_ge(s_bnz, 2)
            S.activation(bnz[:, 2:3], bnz[:, 1:2], ACT.Sqrt, bias=eps[0:H, :]).then_inc(s_bnz, 1)
            act.wait_ge(s_bnz, 7)

            def z_silu(b, h):
                return S.activation(sta[0:H, h, :], blk(feat, 0, H, b), ACT.Silu, scale=bnz[:, 2:3], bias=bnz[:, 3:4])

            def keep_hop(b, h):
                return S.copy(tiles(hop, b), nod[:, h, 0, :, :])

            turns(act, d_l1, [(1, z_silu), *ln_act(4), (12, keep_resid), (14, take_feat)])
            act.wait_ge(s_pass, 4)
            turns(act, d_l2, [(1, sums_to_sta), *ln_act(4), (12, keep_resid), (14, keep_hop)])
            for k in range(2):
                act.wait_ge(s_pass, 5 + k)
                turns(act, d_hop[k], [(1, sums_to_sta), (5, keep_hop)])
            act.wait_ge(s_pass, 7)
            turns(act, d_hop[2], [(1, sums_to_sta), (6, take_feat), *ln_act(10)])

        @block.tensor
        def _(pe):
            pe.wait_ge(s_lim, 3)
            T.matmul(bank[0][:, 0:P], diag[:, :], ident, start=True, stop=True)
            T.matmul(bank[1][:, 0:P], base_f[:, :], ident, start=True, stop=True).then_inc(s_lim, 1)
            pe.wait_ge(s_lim, 8)
            pe.wait_ge(s_set, 3)
            T.matmul(bank[2][:, 0:P], ones[:, :], diag[:, :], start=True, stop=True)
            T.matmul(bank[3][0:1, 0:P], lim[:, 2:3], ident, start=True, stop=True).then_inc(s_lim, 1)
            pe.wait_ge(s_par, 80)
            n_win = n_windows(pe)

            sum_groups(pe, p_conv1, n_win, lambda h, c: gath[:, h, c, :], gathered(p_conv1), width=P)

            def conv1(b, h):
                for t in range(TB):
                    T.matmul(nb(h, 2)[:, t:t + 1], stb[0:H, h, t * P:(t + 1) * P], ident[0:H, 0:1],
                             start=True, stop=True)
                for j in range(2):
                    last = T.matmul(nb(h, j)[0:H, 0:HB], wts[:, W_CONV1, :], blk(feat, 0, P, b, j),
                                    start=True, stop=True)
                return last

            def mlp1(b, h):
                for j in range(2):
                    last = T.matmul(nb(h, 2 + j)[0:H, 0:HB], wts[0:H, W_MLP1, :], halves(sta, h, 0, H)[j],
                                    start=True, stop=True)
                return last

            def mlp2(b, h):
                for t in range(TB):
                    T.matmul(nb(h, 2)[:, t * H:(t + 1) * H], stb[0:H, h, t * P:(t + 1) * P], wts[0:H, W_MLP2, :],
                             start=True, stop=True)
                for j in range(2):
                    last = T.matmul(nb(h, j)[:, 0:HB], wts[0:H, W_MLP2:W_MLP2 + 2, :].rearrange("p a f -> p (a f)"),
                                    halves(stb, h, 0, H)[j], start=True, stop=True)
                return last

            open_turns(pe, d_conv1)
            pe.wait_ge(s_xf, 16)
            turns(pe, d_conv1, [(5, conv1), (8, mlp1), (10, mlp2)])

            sum_groups(pe, p_conv2, n_win, lambda h, c: gath[:, h, c, 0:H], gathered(p_conv2))

            def conv2(b, h):
                for t in range(TB):
                    last = T.matmul(nb(h, 0)[:, t * H:(t + 1) * H], sta[:, h, t * P:(t + 1) * P], wts[:, W_CONV2, :],
                                    start=True, stop=True)
                return last

            open_turns(pe, d_conv2)
            turns(pe, d_conv2, [(3, conv2), (15, node_by_feat(1)), (18, times_w(W_L1X))])

            with pe.Fori(0, ITERS) as i:
                for h in range(2):
                    hold(pe, s_ef[h], 16 * (i + 1))
                    hold(pe, s_eh, 2 * i + h + 1)
                    for c in range(C):
                        half, at = divmod(c, CA)
                        last = T.matmul(bank[2 * h + half][:, at * H:(at + 1) * H],
                                        eft[half * H:(half + 1) * H, h, at * P:(at + 1) * P],
                                        wts[half * H:(half + 1) * H, W_L1E, :], start=True, stop=True)
                    last.then_inc(s_emm, 1)
            pe.wait_ge(s_eacc[0], GROUPS + 1)
            pe.wait_ge(s_eacc[1], GROUPS + 2)
            for j in range(2):
                for c in range(C):
                    last = T.matmul(bank[4 + j][:, 0:H], ones[:, :], accum[:, j, c, :], start=(c == 0), stop=(c == C - 1))
            last.then_inc(s_bn, 1)
            sum_groups(pe, p_msg, n_win, lambda h, c: emsg[:, h, c, :],
                       lambda pe, k, h: hold(pe, s_msg, 2 * k + h + 3))

            def zlin(b, h):
                for j in range(2):
                    last = T.matmul(nb(h, j)[0:H, 0:HB], wts[:, W_L1Z, :], blk(feat, 0, P, b, j), start=True, stop=True)
                return last

            open_turns(pe, d_z)
            turns(pe, d_z, [(2, zlin)])
            open_turns(pe, d_l1)
            turns(pe, d_l1, [(2, feat_by_node), (13, node_by_feat(1)), (15, times_w(W_L2))])
            sum_groups(pe, p_att, n_win, lambda h, c: gath[:, h, c, 0:H], gathered(p_att))
            open_turns(pe, d_l2)
            turns(pe, d_l2, [(2, feat_by_node)])
            for k in range(3):
                sum_groups(pe, p_hop[k], n_win, lambda h, c: gath[:, h, c, 0:H], gathered(p_hop[k]))
                open_turns(pe, d_hop[k])
                turns(pe, d_hop[k], [(2, feat_by_node)] + ([(5, node_by_feat(1)), (7, times_w(W_L3))] if k == 2 else []))

        @block.vector
        def _(dve):
            dve.wait_ge(s_dst, 32)
            V.tensor_copy(dst_f[:, :, :].rearrange("p g c -> p (g c)"),
                          wide[:, 0:C * GROUPS].bitcast(i32)).then_inc(s_lim, 1)
            dve.wait_ge(s_lim, 1)
            V.tensor_reduce(diag[:, :], dst_f[:, :, :], AX.X, ALU.min).then_inc(s_lim, 1)
            V.tensor_reduce(base_f[:, :], dst_f[:, :, :], AX.X, ALU.max).then_inc(s_lim, 1)
            dve.wait_ge(s_lim, 4)
            V.tensor_reduce(lim[:, 0:1], bank[0][:, 0:P], AX.X, ALU.min).then_inc(s_lim, 1)
            V.tensor_reduce(lim[:, 1:2], bank[1][:, 0:P], AX.X, ALU.max).then_inc(s_lim, 1)
            dve.wait_ge(s_lim, 6)
            V.tensor_tensor(lim[:, 2:3], lim[:, 1:2], lim[:, 0:1], ALU.subtract).then_inc(s_lim, 1)
            V.tensor_scalar(diag[:, :], ident, lim[:, 0:1], None, ALU.mult).then_inc(s_lim, 1)
            dve.wait_ge(s_lim, 9)
            V.tensor_copy(base_f[:, :], bank[2][:, 0:P]).then_inc(s_lim, 1)
            V.tensor_copy(base_i[:, :], bank[2][0:1, 0:P]).then_inc(s_lim, 1)
            V.tensor_reduce(lim[0:1, 3:4], bank[3][0:1, 0:P], AX.X, ALU.max).then_inc(s_lim, 1)
            dve.wait_ge(s_lim, 12)
            V.tensor_copy(span_i[:, :], lim[0:1, 3:4]).then_inc(s_lim, 1)
            V.tensor_tensor(dst_f[:, :, :], dst_f[:, :, :],
                            base_f[:, :].rearrange("p (g o) -> p g o", o=1).to_broadcast([P, GROUPS, C]),
                            ALU.subtract).then_inc(s_lim, 1)
            dve.wait_ge(s_lim, 14)
            dve.sem_inc(s_win, 1)
            n_win = n_windows(dve)

            add_windows(dve, p_conv1, n_win, width=P)

            def take_degree(b, h):
                return V.tensor_copy(stb[0:H, h, :], blk(rdeg, 0, H, b))

            def degree_max(b, h):
                return V.tensor_scalar(blk(rdeg, 0, H, b), blk(rdeg, 0, H, b), 1.0, None, ALU.max)

            def degree_inv(b, h):
                return V.reciprocal(blk(rdeg, 0, H, b), blk(rdeg, 0, H, b))

            def mean(b, h):
                return V.tensor_tensor(blk(feat, 0, H, b), blk(feat, 0, H, b), blk(rdeg, 0, H, b), ALU.mult)

            def degree_by_node(b, h):
                return V.tensor_copy(deg_n[:, bass.ds(b * TB, TB)], nb(h, 2)[:, 0:TB])

            def plus_row(d, j, r):
                def work(b, h):
                    stored(dve, d, b, h)
                    return V.tensor_tensor(nod[:, h, 0, :, :], nodes(h, j), row_b(r), ALU.add)
                return work

            dve.wait_ge(s_deg, 16)
            turns(dve, d_conv1, [(1, take_degree), (2, degree_max), (3, degree_inv), (4, mean), (6, degree_by_node),
                                 (12, plus_row(d_conv1, 2, R_B2))])
            for h in range(2):
                dve.wait_ge(d_conv1.turn[h], DITERS * d_conv1.steps + 1)
            V.tensor_scalar(deg_n[:, :], deg_n[:, :], 1.0, None, ALU.add).then_inc(s_dg, 1)
            dve.wait_ge(s_dg, 1)
            V.reciprocal(dinv2[:, :], deg_n[:, :]).then_inc(s_dg, 1)

            add_windows(dve, p_conv2, n_win)

            def mean_to_sta(b, h):
                return V.tensor_tensor(sta[0:H, h, :], blk(feat, 0, H, b), blk(rdeg, 0, H, b), ALU.mult)

            def plus_bias(r):
                def work(b, h):
                    return V.tensor_tensor(nod[:, h, 1, :, :], nod[:, h, 1, :, :], row_b(r), ALU.add)
                return work

            def clear_padding(b, h):
                return V.tensor_tensor(nod[:, h, 0, :, :], nod[:, h, 0, :, :], by_tile(val, b), ALU.mult)

            dve.wait_ge(s_par, 80)
            turns(dve, d_conv2, [(1, mean_to_sta), (4, add_resid), (5, plus_bias(R_BL2)), *ln_dve(6), (13, ln_scale(1)),
                                 (19, plus_row(d_conv2, 3, R_B1)), (20, clear_padding)])

            V.memset(accum[:, :, :, :], 0.0).then_inc(s_eacc[0], 1)
            dve.wait_ge(s_eacc[0], 1)
            dve.sem_inc(s_eacc[1], 2)
            dve.sem_inc(s_eh, 2)
            with dve.Fori(0, ITERS) as i:
                for h in range(2):
                    q = 2 * i + h
                    hold(dve, p_edge.rows_in[h], 16 * C * (i + 1))
                    hold(dve, s_emm, q + 1)
                    hold(dve, s_est[h], 16 * i + 16)
                    for half, (lo, hi) in enumerate(((0, CA), (CA, C))):
                        last = V.tensor_tensor(
                            ebuf[:, h, lo:hi, :], gath[:, h, lo:hi, 0:H],
                            bank[2 * h + half][:, 0:(hi - lo) * H].rearrange("p (c f) -> p c f", f=H), ALU.add)
                    last.then_inc(s_eh, 1)
                    hold(dve, s_eh, q + 3)
                    hold(dve, s_eacc[0], q + 1)
                    V.tensor_tensor(accum[:, 0, :, :], accum[:, 0, :, :], ebuf[:, h, :, :], ALU.add)\
                        .then_inc(s_eacc[0], 1)
                for h in range(2):
                    q = 2 * i + h
                    hold(dve, s_esq, q + 1)
                    hold(dve, s_eacc[1], q + 2)
                    V.tensor_tensor(accum[:, 1, :, :], accum[:, 1, :, :], emsg[:, h, :, :], ALU.add)\
                        .then_inc(s_eacc[1], 1)
            dve.wait_ge(s_bn, 1)
            V.tensor_scalar(bn[:, 0, :], bank[4][:, 0:H], 1.0 / E, None, ALU.mult).then_inc(s_bn, 1)
            V.tensor_scalar(bn[:, 1, :], bank[5][:, 0:H], 1.0 / E, None, ALU.mult).then_inc(s_bn, 1)
            dve.wait_ge(s_bn, 3)
            V.tensor_tensor(bn[:, 2, :], bn[:, 0, :], bn[:, 0, :], ALU.mult).then_inc(s_bn, 1)
            dve.wait_ge(s_bn, 4)
            V.tensor_tensor(bn[:, 1, :], bn[:, 1, :], bn[:, 2, :], ALU.subtract).then_inc(s_bn, 1)
            dve.wait_ge(s_bn, 6)
            V.reciprocal(bn[:, 2, :], bn[:, 2, :]).then_inc(s_bn, 1)
            dve.wait_ge(s_bn, 7)
            V.tensor_tensor(bn[:, 1, :], bn[:, 2, :], row[:, R_G1, :], ALU.mult).then_inc(s_bn, 1)
            dve.wait_ge(s_bn, 8)
            V.tensor_tensor(bn[:, 2, :], bn[:, 0, :], bn[:, 1, :], ALU.mult).then_inc(s_bn, 1)
            dve.wait_ge(s_bn, 9)
            V.tensor_tensor(bn[:, 3, :], row[:, R_BE1, :], bn[:, 2, :], ALU.subtract).then_inc(s_bn, 1)
            dve.wait_ge(s_bn, 10)

            def shift_acts(dve, k, h):
                hold(dve, s_mul, 2 * k + h + 1)
                V.tensor_tensor(ebuf[:, h, :, :], ebuf[:, h, :, :], bn[:, 3:4, :].to_broadcast([P, C, H]), ALU.add)\
                    .then_inc(s_mad, 1)

            add_windows(dve, p_msg, n_win, scale=shift_acts)

            def z_stats(b, h):
                for j in range(2):
                    last = V.bn_stats(stats[:, bass.ds(2 * b + j, 1), :].rearrange("p a s -> p (a s)"),
                                      blk(feat, 0, H, b, j))
                return last

            turns(dve, d_z, [(1, mean), (4, z_stats)])
            for h in range(2):
                dve.wait_ge(d_z.turn[h], DITERS * d_z.steps + 1)
            V.bn_stats(stats[:, 2 * NB - 1, :], feat[0:H, NP - HB:N]).then_inc(s_bnz, 1)
            dve.wait_ge(s_bnz, 1)
            V.bn_aggr(bnz[:, 0:2], stats[:, :, :].rearrange("p a s -> p (a s)")).then_inc(s_bnz, 1)
            dve.wait_ge(s_bnz, 3)
            V.reciprocal(bnz[:, 2:3], bnz[:, 2:3]).then_inc(s_bnz, 1)
            dve.wait_ge(s_bnz, 4)
            V.tensor_tensor(bnz[:, 2:3], bnz[:, 2:3], col[0:H, C_G2:C_G2 + 1], ALU.mult).then_inc(s_bnz, 1)
            dve.wait_ge(s_bnz, 5)
            V.tensor_tensor(bnz[:, 1:2], bnz[:, 0:1], bnz[:, 2:3], ALU.mult).then_inc(s_bnz, 1)
            dve.wait_ge(s_bnz, 6)
            V.tensor_tensor(bnz[:, 3:4], col[0:H, C_BE2:C_BE2 + 1], bnz[:, 1:2], ALU.subtract).then_inc(s_bnz, 1)

            turns(dve, d_l1, [(3, add_resid), *ln_dve(4), (11, ln_scale(1)), (16, plus_row(d_l1, 3, R_HB))])
            dve.wait_ge(s_att, 16)
            add_windows(dve, p_att, n_win, weigh=True)

            def first_hop(b, h):
                stored(dve, d_l2, b, h)
                return V.tensor_tensor(nod[:, h, 0, :, :], nod[:, h, 1, :, :], by_tile(dinv, b), ALU.mult)

            dve.wait_ge(s_dg, 3)
            turns(dve, d_l2, [(3, add_resid), *ln_dve(4), (11, ln_scale(1)), (13, first_hop)])

            def plus_self(b, h):
                return V.tensor_tensor(nod[:, h, 1, :, :], nodes(h, 0), tiles(hop, b), ALU.add)

            def next_hop(d):
                def work(b, h):
                    stored(dve, d, b, h)
                    return V.tensor_tensor(nod[:, h, 0, :, :], nod[:, h, 1, :, :], by_tile(dinv2, b), ALU.mult)
                return work

            def last_hop(b, h):
                return V.tensor_tensor(nod[:, h, 1, :, :], nod[:, h, 1, :, :], by_tile(dinv, b), ALU.mult)

            def result(b, h):
                stored(dve, d_hop[2], b, h)
                return ln_scale(0)(b, h)

            for k in range(2):
                add_windows(dve, p_hop[k], n_win)
                turns(dve, d_hop[k], [(3, plus_self), (4, next_hop(d_hop[k]))])
            add_windows(dve, p_hop[2], n_win)
            turns(dve, d_hop[2], [(3, plus_self), (4, last_hop), (8, lambda b, h: add_resid(b, h, 3)),
                                  (9, plus_bias(R_B3)), *ln_dve(10), (17, result)])


def kernel(**inputs):
    import numpy as _np
    import concourse.bacc as _bacc
    from concourse import mybir as _mybir
    from concourse.bass_utils import run_bass_kernel_spmd as _run

    a = {k: _np.asarray(v) for k, v in inputs.items()}
    f = _np.float32
    ep = GROUPS * C * P
    x_rows = _np.zeros((NP, H), f)
    x_rows[:N] = a["x"]

    def lists(v, fill):
        p = _np.full((ep,), fill, v.dtype)
        p[:E] = v.reshape(E)
        return p.reshape(GROUPS, C, P)

    edges = _np.zeros((ep, H), f)
    edges[:E] = a["edge_attr_64"]
    edges = edges.reshape(GROUPS, C, P, H)
    edge_feat = _np.zeros((GROUPS, 2, H, CA, P), f)
    edge_feat[:, 0] = edges[:, :CA].transpose(0, 3, 1, 2)
    edge_feat[:, 1, :, :CB] = edges[:, CA:].transpose(0, 3, 1, 2)

    w = _np.zeros((P, 10, H), f)
    w[:H, W_CONV1], w[H:, W_CONV1] = a["L0_gnn_conv1_Wl"].T, a["L0_gnn_conv1_Wr"].T
    w[:H, W_MLP1] = a["L0_gnn_mlp_W1"].T
    w[:H, W_MLP2] = w[:H, W_MLP2 + 1] = a["L0_gnn_mlp_W2"].T
    w[:H, W_CONV2], w[H:, W_CONV2] = a["L0_gnn_conv2_Wl"].T, a["L0_gnn_conv2_Wr"].T
    w[H:, W_L1X] = a["L1_gnn_W1"][:H]
    w[:H, W_L1E] = w[H:, W_L1E] = a["L1_gnn_W1"][H:]
    w[:H, W_L1Z], w[H:, W_L1Z] = a["L1_gnn_W2"][H:], a["L1_gnn_W2"][:H]
    w[H:, W_L2] = a["L2_gnn_weight"]
    w[H:, W_L3] = a["L3_gnn_W"]
    cols = _np.stack([_np.concatenate([a[k], a[k]]) for k in (
        "L0_gnn_conv1_bl", "L0_gnn_mlp_b1", "L0_gnn_mlp_b2", "L1_gnn_b2", "L1_gnn_g2", "L1_gnn_be2")], axis=1)
    rows = _np.stack([a[k] for k in (
        "L0_gnn_mlp_b2", "L0_gnn_conv2_bl", "L1_gnn_b1", "L2_gnn_h_bias", "L3_gnn_b", "L1_gnn_g1", "L1_gnn_be1")])
    rows = _np.broadcast_to(rows, (P,) + rows.shape)
    consts = _np.stack([_np.eye(P, dtype=f), _np.broadcast_to(_np.arange(P, dtype=f), (P, P))], axis=1)
    valid = (_np.arange(NP) < N).astype(f).reshape(NT, P).T

    arrays = dict(
        x_rows=x_rows, x_feat=x_rows.T, src_idx=lists(a["src"], N).transpose(0, 2, 1),
        dst_idx=lists(a["dst"], N).transpose(2, 0, 1).reshape(P, GROUPS * C),
        att=lists(a["edge_weight1"], 0).transpose(2, 0, 1), edge_feat=edge_feat.reshape(GROUPS, P, CA * P),
        consts=consts, valid=valid, weights=w, cols=cols, rows=rows)
    nc = _bacc.Bacc("TRN2", target_bir_lowering=False, num_devices=1)
    arrays = {k: _np.ascontiguousarray(v) for k, v in arrays.items()}
    aps = [nc.dram_tensor(k, v.shape, _mybir.dt.from_np(v.dtype), kind="ExternalInput").ap() for k, v in arrays.items()]
    out = nc.dram_tensor("out_rows", (NP, H), _mybir.dt.float32, kind="ExternalOutput").ap()
    gnn_program(nc, *aps, out)
    r = _run(nc, [arrays], core_ids=[0])
    return r.results[0]["out_rows"][:N]
```

```python
import concourse.bass as bass
from concourse import mybir
from contextlib import ExitStack

P = 128
N = 12500
E = 212500
H = 64
NT = -(-N // P)
NP = NT * P
C = 13
GROUPS = -(-E // (P * C))
ITERS = GROUPS // 2
CA = (C + 1) // 2
CB = C - CA
W = 128
TB = 7
NB = NT // TB
BN = TB * P
HB = BN // 2
DITERS = NB // 2
EPS = 1e-5
D = 4
BT = P // D
BLOCKS = NT * BT
FC = -(-(GROUPS * C * P + P) // P // 4) * 4
TITERS = NT // 2
NO_NODE = 1 << 14
MAX_COUNT = 16.0
assert GROUPS == P and NB * TB == NT and NB % 2 == 0

W_CONV1, W_MLP1, W_MLP2, W_CONV2, W_L1X, W_L1E, W_L1Z, W_L2, W_L3 = 0, 1, 2, 4, 5, 6, 7, 8, 9
C_BL1, C_B1, C_B2, C_BZ, C_G2, C_BE2 = range(6)
R_B2, R_BL2, R_B1, R_HB, R_B3, R_G1, R_BE1 = range(7)


def gnn_program(nc, x_rows, x_feat, src_idx, dst_idx, src_flat, dst_flat, att, edge_feat, consts, valid, weights,
                cols, rows, out):
    f32, i32 = mybir.dt.float32, mybir.dt.int32
    bf16, f16, f8 = mybir.dt.bfloat16, mybir.dt.float16, mybir.dt.float8e4
    ALU, ACT, AX = mybir.AluOpType, mybir.ActivationFunctionType, mybir.AxisListType
    V, S, T = nc.vector, nc.scalar, nc.tensor
    ctx = ExitStack()
    with ctx:
        def sb(name, shape, dt=f32):
            return ctx.enter_context(nc.sbuf_tensor(name, shape, dt))

        def sem(name):
            return ctx.enter_context(nc.semaphore(name))

        def sems(name, n=2):
            return [sem(f"{name}{i}") for i in range(n)]

        def dram(name, shape):
            return nc.dram_tensor(name, shape, f32, kind="Internal").ap()

        tab_h2, tab_l1, tab_l2 = dram("tab_h2", [NP, H]), dram("tab_l1", [NP, H]), dram("tab_l2", [NP, H])
        tab_hop = [dram(f"tab_hop{k}", [NP, H]) for k in range(3)]
        edge_h = dram("edge_h", [GROUPS, P, C * H])
        record = dram("record", [P * FC, 3])
        first_edge = nc.dram_tensor("first_edge", [1, BLOCKS], i32, kind="Internal").ap()
        counts = nc.dram_tensor("counts", [NT, P, NT * P // 4], f32, kind="Internal").ap()

        feat = sb("feat", [P, NP + W])
        wide = sb("wide", [P, NP])
        rdeg = wide[0:H, :]
        att_s = wide[:, NP - GROUPS * C:NP].rearrange("p (g c) -> p g c", c=C)
        resid = sb("resid", [P, NT, H])
        hop = wide[:, 0:NT * H].rearrange("p (t f) -> p t f", f=H)
        dst_f = sb("dst_f", [P, GROUPS, C])
        idx = sb("idx", [P, 2, C], i32)
        gath = sb("gath", [P, 2, C, 2 * H])
        oneh = sb("oneh", [P, 2, C, W])
        area = sb("area", [P, 2 * BN + 2 * BN + 6 * TB * H + 2 * C * H])
        accum = area[:, 4 * BN + 6 * TB * H:].rearrange("p (s c f) -> p s c f", s=2, f=H)
        cst = sb("cst", [P, 2, P])
        WT, WS, WD, WU, WR = 0, FC, 2 * FC, 3 * FC, 4 * FC
        assert 7 * FC <= NP
        ident, iota0 = cst[:, 0, :], cst[:, 1, :]
        val = sb("val", [P, NT])
        iota_w = sb("iota_w", [P, 1, W])
        ones = sb("ones", [P, P])
        wts = sb("wts", [P, weights.shape[1], H])
        col = sb("col", [P, cols.shape[1]])
        row = sb("row", [P, rows.shape[1], H])
        lim = sb("lim", [P, 4])
        diag = sb("diag", [P, P])
        base_f = sb("base_f", [P, GROUPS])
        base_i = sb("base_i", [1, GROUPS], i32)
        base_w = sb("base_w", [1, GROUPS], i32)
        first_i = oneh[H:H + 1, :, :, :].rearrange("p s c w -> p (s c w)")[:, 0:BLOCKS].bitcast(i32)
        span_i = sb("span_i", [1, 1], i32)
        deg_n = sb("deg_n", [P, NT])
        dinv = sb("dinv", [P, NT])
        dinv2 = sb("dinv2", [P, NT])
        bn = sb("bn", [P, 4, H])
        bnz = sb("bnz", [H, 4])
        stats = sb("stats", [H, 2 * NB, 6])
        sta = area[:, 0:2 * BN].rearrange("p (s n) -> p s n", s=2)
        stb = area[:, 2 * BN:4 * BN].rearrange("p (s n) -> p s n", s=2)
        nod = area[:, 4 * BN:4 * BN + 6 * TB * H].rearrange("p (s a t f) -> p s a t f", s=2, a=3, f=H)
        ln = sb("ln", [P, 2, 3, TB])
        eft = sta
        ebuf = stb[:, :, 0:C * H].rearrange("p s (c f) -> p s c f", f=H)
        emsg = area[:, 4 * BN:4 * BN + 6 * TB * H].rearrange("p (s n) -> p s n", s=2)[:, :, 0:C * H]\
            .rearrange("p s (c f) -> p s c f", f=H)
        TW = NT * P // 4
        slab = [area[:, u * TW:(u + 1) * TW] for u in range(2)]
        pair_oh = area[:, 2 * TW:2 * TW + 8 * NT * D // 2].bitcast(bf16).rearrange("p (b n) -> p b n", b=8)
        low_oh = sb("low_oh", [P, 8, P], bf16)
        rec = sb("rec", [P, 2, BT, 3])
        key = sb("key", [P, 2, BT])
        first_w = sb("first_w", [1, 2, BT], i32)
        blk_w = sb("blk_w", [P, 2, BT])
        wide_iota = sb("wide_iota", [P, NT * D], f16)
        cells = sb("cells", [P, 2, BT // 2])
        caught = sb("caught", [P, 2, NT])
        chk = sb("chk", [P, 4])
        ok_i = sb("ok_i", [1, 1], i32)
        ident_b = sb("ident_b", [P, P], bf16)
        tile_in = [t[:, :, :, :].rearrange("p s c w -> p (s c w)")[:, 0:TW] for t in (gath, oneh)]
        parts = [t[:, 0:NT * 3 * H // 2].bitcast(bf16).rearrange("p (t a f) -> p t a f", a=3, f=H) for t in (wide, feat)]
        hsum = feat[:, 0:NT * H].rearrange("p (t f) -> p t f", f=H)
        eps = sb("eps", [P, 1])

        banks = ctx.enter_context(nc.psum_tensor("banks", [P, 8, 512], f32))
        bank = [banks[:, i, :] for i in range(8)]
        window = [bank[7 * h][:, 0:W] for h in range(2)]

        s_dst, s_par, s_att, s_xf, s_deg = sem("dst_in"), sem("params_in"), sem("att_in"), sem("xfeat_in"), sem("deg_moved")
        s_set = sem("constants_set")
        s_lim = sem("setup_steps")
        s_win = sem("windows_known")
        s_gate = sem("gate")
        s_pre = sem("pass_prepared")
        s_shift = sem("windows_shifted")
        s_pass = sem("pass_done")
        s_table = sem("table_stored")
        s_weighed = sem("onehots_placed")

        def hold(eng, s, value):
            eng.wait_ge(s, value)
            eng.sem_inc(s_gate, 1)

        class Pass:

            def __init__(self, name, gathers=True, sums=True):
                if gathers:
                    self.idx_in = sems(f"{name}_idx_in")
                    self.rows_in = sems(f"{name}_rows_in")
                if not sums:
                    return
                self.onehot = sem(f"{name}_onehot")
                self.summed = sem(f"{name}_summed")
                self.added = sem(f"{name}_added")

        p_conv1, p_conv2, p_att = (Pass(n) for n in ("conv1", "conv2", "att"))
        p_edge, p_msg = Pass("edge", sums=False), Pass("msg", gathers=False)
        p_hop = [Pass(f"hop{k}") for k in range(3)]
        s_ef = sems("edge_feat_in")
        s_emm = sem("edge_product")
        s_eh = sem("edge_act")
        s_esq = sem("edge_squared")
        s_eacc = sems("edge_accumulated")
        s_est = sems("edge_stored")
        s_hl, s_mul = sems("act_loaded"), sem("act_scaled")
        s_mad, s_msg = sem("act_shifted"), sem("message")
        s_rec, s_first = sem("records"), sem("first_edges")
        b_first = sems("b_first_in")
        b_rec = sems("b_records_in")
        b_key = sem("b_keys")
        b_tmp, b_again, b_red = sem("b_steps"), sem("b_again"), sem("b_cells_read")
        b_oh, b_mm, b_ev = sem("b_onehots"), sem("b_products"), sem("b_counts")
        b_st = sems("b_stored")
        s_ok_in, s_ok = sem("counts_check_steps"), sem("counts_checked")
        h_in = [sems(f"h{k}_tile_in") for k in range(3)]
        h_mm, h_red, h_dve = sems("h_product", 3), sems("h_summed", 3), sems("h_steps", 3)
        s_bn, s_bnz, s_dg = sem("bn_steps"), sem("bnz_steps"), sem("degree_steps")

        class Turns:

            def __init__(self, name, steps, stores=True):
                self.turn, self.steps = sems(f"{name}_turn"), steps
                if stores:
                    self.stored = sems(f"{name}_stored")

            def wait(self, eng, i, h, step):
                hold(eng, self.turn[h], i * self.steps + step)

        def done(ins, d, h):
            ins.then_inc(d.turn[h], 1)

        d_conv1, d_conv2, d_z, d_l1, d_l2 = (Turns("d_conv1", 12), Turns("d_conv2", 20), Turns("d_z", 4, stores=False),
                                             Turns("d_l1", 16), Turns("d_l2", 14))
        d_l2d, d_out = Turns("d_l2d", 18, stores=False), Turns("d_out", 14)
        d_hop = [Turns("d_hop0", 5), Turns("d_hop1", 5), Turns("d_hop2", 17)]

        block = ctx.enter_context(nc.Block())

        def n_windows(eng):
            eng.wait_ge(s_win, 1)
            return eng.value_load(span_i[0:1, 0:1], min_val=0, max_val=NP) // W + 1

        def group(t, g):
            return t[bass.ds(g, 1), :, :].rearrange("a p c -> (a p) c")

        def steps(eng, side, w):
            if side is None:
                yield (0, ITERS), lambda i, u: None
            else:
                yield (0, TITERS), lambda i, u: side(w * TITERS + i, i, u)
                yield (TITERS, ITERS), lambda i, u: None

        def load_lists(sp, p, n_win, used, edge=False, side=None):
            with sp.Fori(0, n_win) as w:
              for (lo, hi), extra in steps(sp, side, w):
                with sp.Fori(lo, hi) as i:
                    for h in range(2):
                        hold(sp, used, 2 * (w * ITERS + i) + h + 1)
                        sp.dma_start(idx[:, h, :], group(src_idx, 2 * i + h)).then_inc(p.idx_in[h], 16)
                        if edge:
                            sp.dma_start(eft[:, h, :], group(edge_feat, 2 * i + h)).then_inc(s_ef[h], 16)
                    for u in range(2):
                        extra(i, u)

        def gather(pool, p, n_win, table):
            with pool.Fori(0, n_win) as w:
                with pool.Fori(0, ITERS) as i:
                    for h in range(2):
                        hold(pool, p.idx_in[h], 16 * (w * ITERS + i + 1))
                        for c in range(C):
                            pool.indirect_dma_start(
                                out=gath[:, h, c, 0:H], out_offset=None, in_=table[:, :],
                                in_offset=bass.IndirectOffsetOnAxis(ap=idx[:, h, c:c + 1], axis=0),
                            ).then_inc(p.rows_in[h], 16)

        def sum_groups(pe, p, n_win, rows_of, rows_are_in, width=H, side=None):
            pe.sem_inc(p.summed, 2)
            with pe.Fori(0, n_win) as w:
              for (lo, hi), extra in steps(pe, side, w):
                with pe.Fori(lo, hi) as i:
                    for h in range(2):
                        q = 2 * (w * ITERS + i) + h
                        rows_are_in(pe, w * ITERS + i, h)
                        hold(pe, p.onehot, q + 1)
                        hold(pe, p.added, q + 1)
                        for c in range(C):
                            last = T.matmul(window[h][0:width, :], rows_of(h, c), oneh[:, h, c, :],
                                            start=(c == 0), stop=(c == C - 1))
                        last.then_inc(p.summed, 1)
                        extra(i, h)

        def gathered(p):
            return lambda pe, k, h: hold(pe, p.rows_in[h], 16 * C * (k + 1))

        passes = [0]

        def add_windows(dve, p, n_win, width=H, weigh=False, scale=None, side=None, after_side=None):
            V.memset(feat[0:width, :], 0.0).then_inc(s_pre, 1)
            V.tensor_copy(iota_w[:, 0, :], iota0).then_inc(s_pre, 1)
            V.tensor_copy(base_w[:, :], base_i[:, :]).then_inc(s_pre, 1)
            before = passes[0]
            passes[0] += 1
            dve.wait_ge(s_pre, 3 * passes[0])
            dve.sem_inc(p.added, 2)
            with dve.Fori(0, n_win) as w:
              for (lo, hi), extra in steps(dve, side, w):
                with dve.Fori(lo, hi) as i:
                    for h in range(2):
                        q = 2 * (w * ITERS + i) + h
                        if scale is not None:
                            scale(dve, w * ITERS + i, h)
                        hold(dve, p.summed, q + 1)
                        ins = V.tensor_tensor(
                            oneh[:, h, :, :], iota_w[:, :, :].to_broadcast([P, C, W]),
                            dst_f[:, bass.ds(2 * i + h, 1), :].rearrange("p a (c o) -> p (a c) o", o=1)
                            .to_broadcast([P, C, W]), ALU.is_equal)
                        if weigh:
                            ins.then_inc(s_weighed, 1)
                            hold(dve, s_weighed, q + 1)
                            ins = V.tensor_tensor(
                                oneh[:, h, :, :], oneh[:, h, :, :],
                                att_s[:, bass.ds(2 * i + h, 1), :].rearrange("p a (c o) -> p (a c) o", o=1)
                                .to_broadcast([P, C, W]), ALU.mult)
                        ins.then_inc(p.onehot, 1)
                    for h in range(2):
                        q = 2 * (w * ITERS + i) + h
                        first = dve.value_load(base_w[0:1, bass.ds(2 * i + h, 1)], min_val=0, max_val=NP)
                        hold(dve, p.summed, q + 3)
                        hold(dve, p.added, q + 2)
                        V.tensor_tensor(feat[0:width, bass.ds(first, W)], feat[0:width, bass.ds(first, W)],
                                        window[h][0:width, :], ALU.add).then_inc(p.added, 1)
                        extra(i, h)
              hold(dve, p.added, 2 * ITERS * (w + 1) + 2)
              V.tensor_scalar(iota_w[:, 0, :], iota_w[:, 0, :], float(W), None, ALU.add).then_inc(s_shift, 1)
              V.tensor_scalar(base_w[:, :], base_w[:, :], float(W), float(NP), ALU.add, ALU.min)\
                  .then_inc(s_shift, 1)
              hold(dve, s_shift, 2 * (n_win * before + w + 1))
              if after_side is not None:
                  after_side(w)
            dve.sem_inc(s_pass, 1)

        def blk(t, lo, hi, b, half=None):
            if half is None:
                return t[lo:hi, bass.ds(b * BN, BN)]
            return t[lo:hi, bass.ds(b * BN + half * HB, HB)]

        def tiles(t, b):
            return t[:, bass.ds(b * TB, TB), :]

        def by_tile(t, b):
            return t[:, bass.ds(b * TB, TB)].rearrange("p (t o) -> p t o", o=1).to_broadcast([P, TB, H])

        def over_features(t):
            return t.rearrange("p (t o) -> p t o", o=1).to_broadcast([P, TB, H])

        def row_b(r):
            return row[:, r:r + 1, :].to_broadcast([P, TB, H])

        def nb(h, j):
            return bank[4 * h + j]

        def nodes(h, j):
            return nb(h, j)[:, 0:TB * H].rearrange("p (t f) -> p t f", t=TB)

        def halves(t, h, lo, hi):
            return [t[lo:hi, h, j * HB:(j + 1) * HB] for j in range(2)]

        def turns(eng, d, steps):
            with eng.Fori(0, DITERS) as i:
                for step, work in steps:
                    for h in range(2):
                        d.wait(eng, i, h, step)
                        done(work(2 * i + h, h), d, h)

        def open_turns(pe, d):
            for h in range(2):
                pe.sem_inc(d.turn[h], 1)

        def store(sp, d, table):
            for h in range(2):
                sp.sem_inc(d.stored[h], 16)
            with sp.Fori(0, DITERS) as i:
                for h in range(2):
                    hold(sp, d.turn[h], (i + 1) * d.steps + 1)
                    sp.dma_start(table[bass.ds((2 * i + h) * BN, BN), :].rearrange("(t p) f -> p t f", p=P),
                                 nod[:, h, 0, :, :]).then_inc(d.stored[h], 16)
            for h in range(2):
                sp.wait_ge(d.stored[h], 16 * DITERS + 16)
            sp.sem_inc(s_table, 1)

        def stored(eng, d, i_block, h):
            hold(eng, d.stored[h], 16 * ((i_block - h) // 2) + 16)

        def feat_by_node(b, h):
            for t in range(TB):
                last = T.matmul(nb(h, 0)[:, t * H:(t + 1) * H], sta[0:H, h, t * P:(t + 1) * P], ident[0:H, 0:H],
                                start=True, stop=True)
            return last

        def node_by_feat(src):
            def work(b, h):
                for t in range(TB):
                    j, at = divmod(t, 4)
                    last = T.matmul(nb(h, 1 + j)[H:P, at * P:(at + 1) * P], nod[:, h, src, t, :], ident,
                                    start=True, stop=True)
                return last
            return work

        def take_feat(b, h):
            S.copy(sta[H:P, h, 0:4 * P], nb(h, 1)[H:P, 0:4 * P])
            return S.copy(sta[H:P, h, 4 * P:BN], nb(h, 2)[H:P, 0:3 * P])

        def times_w(w):
            def work(b, h):
                for t in range(TB):
                    last = T.matmul(nb(h, 3)[:, t * H:(t + 1) * H], sta[H:P, h, t * P:(t + 1) * P], wts[H:P, w, :],
                                    start=True, stop=True)
                return last
            return work

        def sums_to_sta(b, h):
            return S.copy(sta[0:H, h, :], blk(feat, 0, H, b))

        def ln_sum(b, h):
            return V.tensor_reduce(ln[:, h, 0, :], nod[:, h, 1, :, :], AX.X, ALU.add)

        def ln_mean(b, h):
            return V.tensor_scalar(ln[:, h, 0, :], ln[:, h, 0, :], -1.0 / H, None, ALU.mult)

        def ln_center(b, h):
            return V.tensor_tensor(nod[:, h, 1, :, :], nod[:, h, 1, :, :], over_features(ln[:, h, 0, :]), ALU.add)

        def ln_square(b, h):
            return S.activation(nod[:, h, 2, :, :], nod[:, h, 1, :, :], ACT.Square)

        def ln_var(b, h):
            return V.tensor_reduce(ln[:, h, 1, :], nod[:, h, 2, :, :], AX.X, ALU.add)

        def ln_std(b, h):
            return S.activation(ln[:, h, 1, :], ln[:, h, 1, :], ACT.Sqrt, bias=eps[:, :], scale=1.0 / H)

        def ln_rstd(b, h):
            return V.reciprocal(ln[:, h, 1, :], ln[:, h, 1, :])

        def ln_scale(to):
            def work(b, h):
                return V.tensor_tensor(nod[:, h, to, :, :], nod[:, h, 1, :, :], over_features(ln[:, h, 1, :]),
                                       ALU.mult)
            return work

        def keep_resid(b, h):
            return S.copy(tiles(resid, b), nod[:, h, 1, :, :])

        def ln_dve(first):
            return [(first, ln_sum), (first + 1, ln_mean), (first + 2, ln_center), (first + 4, ln_var),
                    (first + 6, ln_rstd)]

        def ln_act(first):
            return [(first + 3, ln_square), (first + 5, ln_std)]

        def add_resid(b, h, j=0):
            return V.tensor_tensor(nod[:, h, 1, :, :], nodes(h, j), tiles(resid, b), ALU.add)

        def counts_sp(sp):
            edge_regs = [sp.alloc_register(f"first_edge{j}") for j in range(16)]

            def side(m, i, u):
                sp.dma_start(first_w[:, u, :], first_edge[0:1, bass.ds((2 * i + u) * BT, BT)]).then_inc(b_first[u], 16)
                hold(sp, b_key, 2 * m + u + 1)
                hold(sp, b_first[u], 16 * (m + 1))
                for q in range(BT // 16):
                    sp.load(edge_regs, first_w[:, u, 16 * q:16 * (q + 1)])
                    for j in range(16):
                        edge = sp.snap(edge_regs[j], min_val=0, max_val=P * FC - P)
                        sp.dma_start(rec[:, u, 16 * q + j, :], record[bass.ds(edge, P), :]).then_inc(b_rec[u], 16)
            return side

        def counts_dve(dve):
            def side(m, i, u):
                hold(dve, b_rec[u], 16 * BT * (m + 1))
                hold(dve, b_tmp, 6 * m + 3 * u + 1)
                V.tensor_tensor(key[:, u, :], rec[:, u, :, 2], blk_w[:, u, :], ALU.not_equal).then_inc(b_tmp, 1)
                hold(dve, b_tmp, 6 * m + 3 * u + 2)
                V.scalar_tensor_tensor(key[:, u, :], key[:, u, :], float(NT * D), rec[:, u, :, 1], ALU.mult, ALU.add)\
                    .then_inc(b_tmp, 1)
                hold(dve, b_tmp, 6 * m + 3 * u + 3)
                V.tensor_scalar(blk_w[:, u, :], blk_w[:, u, :], float(2 * BT), None, ALU.add).then_inc(b_tmp, 1)
                for q in range(BT // 2):
                    dve.wait_ge(b_mm, (2 * m + u) * (BT // 2) + q + 1)
                    for j in range(2):
                        at, ring = 2 * q + j, (2 * q + j) % 8
                        V.tensor_scalar(pair_oh[:, ring, :], wide_iota[:, :], key[:, u, at:at + 1], None, ALU.is_equal)
                        last = V.tensor_scalar(low_oh[:, ring, :], wide_iota[:, 0:P], rec[:, u, at, 0:1], None,
                                               ALU.is_equal)
                    last.then_inc(b_oh, 1)
                hold(dve, b_oh, (2 * m + u + 1) * (BT // 2))
                dve.sem_inc(b_key, 1)
                hold(dve, b_ev, (2 * m + u + 1) * (BT // 2) + 2)
                V.tensor_reduce(caught[:, 0, bass.ds(2 * i + u, 1)], cells[:, u, :], AX.X, ALU.max)
                V.tensor_reduce(caught[:, 1, bass.ds(2 * i + u, 1)], cells[:, u, :], AX.X, ALU.add).then_inc(b_red, 1)
            return side

        def counts_pe(pe):
            def side(m, i, u):
                for q in range(BT // 2):
                    n = (2 * m + u) * (BT // 2) + q
                    pe.wait_ge(b_oh, n + 1)
                    pe.wait_ge(b_ev, n + 1)
                    for j in range(2):
                        ring = (2 * q + j) % 8
                        last = T.matmul(bank[1 + 2 * (q % 2) + j][:, 0:NT * D], low_oh[:, ring, :],
                                        pair_oh[:, ring, :], start=True, stop=True)
                    last.then_inc(b_mm, 1)
            return side

        def counts_act(act):
            def side(m, i, u):
                hold(act, b_st[u], 16 * m + 16)
                hold(act, b_red, 2 * m + u + 1)
                for q in range(BT // 2):
                    bk = 1 + 2 * (q % 2)
                    hold(act, b_mm, (2 * m + u) * (BT // 2) + q + 5)
                    to = slab[u].bitcast(f8).rearrange("p (s n) -> p s n", s=NT)[:, :, 2 * D * q:2 * D * (q + 1)]
                    S.activation(to.rearrange("p s (b d) -> p b s d", d=D),
                                 banks[:, bk:bk + 2, 0:NT * D].rearrange("p b (s d) -> p b s d", d=D),
                                 ACT.Copy, saturate=False, accum_out=cells[:, u, q:q + 1]).then_inc(b_ev, 1)
                hold(act, b_ev, (2 * m + u + 1) * (BT // 2) + 2)
                act.dma_start(counts[bass.ds(2 * i + u, 1), :, :].rearrange("a p n -> (a p) n"), slab[u])\
                    .then_inc(b_st[u], 16)
            return side

        def counts_in(sp, k):
            with sp.Fori(0, TITERS) as i:
                for u in range(2):
                    hold(sp, h_mm[k], 2 * i + u + 1)
                    sp.dma_start(tile_in[u], counts[bass.ds(2 * i + u, 1), :, :].rearrange("a p n -> (a p) n"))\
                        .then_inc(h_in[k][u], 16)

        def times_counts(pe, k, src):
            pe.sem_inc(h_mm[k], 2)
            with pe.Fori(0, TITERS) as i:
                for u in range(2):
                    hold(pe, h_in[k][u], 16 * (i + 1))
                    hold(pe, h_red[k], 2 * i + u + 1)
                    to = bank[u][:, 0:3 * H]
                    T.matmul(to, ident_b[:, :], parts[src][:, bass.ds(2 * i + u, 1), :, :]
                             .rearrange("p t a f -> p (t a f)"), start=True, stop=False)
                    for t in range(NT):
                        last = T.matmul(to, tile_in[u].bitcast(f8)[:, t * P:(t + 1) * P],
                                        parts[src][:, t, :, :].rearrange("p a f -> p (a f)"),
                                        start=False, stop=(t == NT - 1))
                    last.then_inc(h_mm[k], 1)

        def hop_dve(dve, k, to):
            dve.sem_inc(h_red[k], 2)
            per = 6 if to is not None else 2
            with dve.Fori(0, TITERS) as i:
                for u in range(2):
                    at = bass.ds(2 * i + u, 1)
                    b = per * (2 * i + u)
                    hold(dve, h_mm[k], 2 * i + u + 3)
                    V.tensor_reduce(nod[:, u, 0, 0, :], bank[u][:, 0:3 * H].rearrange("p (a f) -> p f a", a=3),
                                    AX.X, ALU.add).then_inc(h_dve[k], 1)
                    hold(dve, h_dve[k], b + 1)
                    dve.sem_inc(h_red[k], 1)
                    if to is None:
                        V.tensor_scalar(hsum[:, at, :].rearrange("p t f -> p (t f)"), nod[:, u, 0, 0, :], dinv[:, at],
                                        None, ALU.mult).then_inc(h_dve[k], 1)
                        continue
                    V.tensor_scalar(nod[:, u, 1, 0, :], nod[:, u, 0, 0, :], dinv2[:, at], None, ALU.mult)\
                        .then_inc(h_dve[k], 1)
                    hold(dve, h_dve[k], b + 2)

                    def part(a):
                        return parts[to][:, at, a, :].rearrange("p t f -> p (t f)")

                    V.tensor_copy(part(0), nod[:, u, 1, 0, :]).then_inc(h_dve[k], 1)
                    hold(dve, h_dve[k], b + 3)
                    V.tensor_tensor(nod[:, u, 1, 0, :], nod[:, u, 1, 0, :], part(0), ALU.subtract).then_inc(h_dve[k], 1)
                    hold(dve, h_dve[k], b + 4)
                    V.tensor_copy(part(1), nod[:, u, 1, 0, :]).then_inc(h_dve[k], 1)
                    hold(dve, h_dve[k], b + 5)
                    V.tensor_tensor(part(2), nod[:, u, 1, 0, :], part(1), ALU.subtract).then_inc(h_dve[k], 1)
            return

        H_STEPS = [12 * TITERS, 12 * TITERS, 4 * TITERS]

        def counts_hold(eng):
            eng.wait_ge(s_ok, 1)
            return eng.value_load(ok_i[0:1, 0:1], min_val=0, max_val=1)

        @block.sync
        def _(sp):
            sp.dma_start(wide[:, 0:C * GROUPS].bitcast(i32), dst_idx)\
                .then_inc(s_dst, 16)
            sp.dma_start(cst[:, :, :], consts).then_inc(s_dst, 16)
            sp.dma_start(wide[:, WS:WS + FC].bitcast(i32), src_flat).then_inc(s_rec, 16)
            sp.dma_start(wide[:, WD:WD + FC].bitcast(i32), dst_flat).then_inc(s_rec, 16)
            for t, src in ((wts[:, :, :], weights), (col[:, :], cols), (row[:, :, :], rows), (val[:, :], valid),
                           (resid[:, :, :], x_rows.rearrange("(t p) f -> p t f", p=P))):
                sp.dma_start(t, src).then_inc(s_par, 16)
            n_win = n_windows(sp)
            sp.wait_ge(s_rec, 39)
            sp.dma_start(record.rearrange("(p c) r -> p (c r)", p=P), wide[:, WR:WR + 3 * FC]).then_inc(s_rec, 16)

            load_lists(sp, p_conv1, n_win, p_conv1.summed)
            sp.wait_ge(s_pass, 1)
            sp.wait_ge(s_rec, 55)
            sp.dma_start(rdeg[:, :], feat[H:P, 0:NP]).then_inc(s_deg, 16)
            sp.wait_ge(s_deg, 16)
            sp.wait_ge(s_first, 3)
            sp.dma_start(first_edge, first_i).then_inc(s_first, 16)
            sp.wait_ge(s_first, 19)
            sp.dma_start(feat[H:P, 0:NP], x_feat).then_inc(s_xf, 16)
            store(sp, d_conv1, tab_h2)
            load_lists(sp, p_conv2, n_win, p_conv2.summed, side=counts_sp(sp))
            store(sp, d_conv2, tab_l1)

            load_lists(sp, p_edge, 1, s_eh, edge=True)
            for h in range(2):
                sp.wait_ge(s_est[h], 16 * ITERS + 16)
            sp.wait_ge(s_bn, 1)
            with sp.Fori(0, n_win) as w:
                with sp.Fori(0, ITERS) as i:
                    for h in range(2):
                        hold(sp, s_msg, 2 * (w * ITERS + i) + h + 1)
                        sp.dma_start(ebuf[:, h, :, :].rearrange("p c f -> p (c f)"),
                                     group(edge_h, 2 * i + h)).then_inc(s_hl[h], 16)
            store(sp, d_l1, tab_l2)
            sp.dma_start(att_s[:, :, :], att).then_inc(s_att, 16)
            load_lists(sp, p_att, n_win, p_att.summed)
            ok = counts_hold(sp)
            with sp.If(ok > 0):
                for u in range(2):
                    hold(sp, b_st[u], 16 * TITERS * n_win + 16)
                for k in range(3):
                    counts_in(sp, k)
                store(sp, d_out, out)
            with sp.Else():
                store(sp, d_l2, tab_hop[0])
                for k in range(3):
                    load_lists(sp, p_hop[k], n_win, p_hop[k].summed)
                    store(sp, d_hop[k], tab_hop[k + 1] if k < 2 else out)

        @block.gpsimd
        def _(pool):
            pool.memset(gath[:, :, :, :], 1.0).then_inc(s_set, 1)
            pool.memset(ones[:, :], 1.0).then_inc(s_set, 1)
            pool.memset(eps[:, :], EPS).then_inc(s_set, 1)
            pool.iota(wide_iota[:, :], pattern=[[1, NT * D]], base=0, channel_multiplier=0,
                      allow_small_or_imprecise_dtypes=True).then_inc(s_set, 1)
            pool.wait_ge(s_set, 4)
            n_win = n_windows(pool)
            gather(pool, p_conv1, n_win, x_rows)
            pool.wait_ge(s_table, 1)
            gather(pool, p_conv2, n_win, tab_h2)
            pool.wait_ge(s_table, 2)
            gather(pool, p_edge, 1, tab_l1)
            pool.wait_ge(s_bn, 10)
            with pool.Fori(0, n_win) as w:
                with pool.Fori(0, ITERS) as i:
                    for h in range(2):
                        hold(pool, s_hl[h], 16 * (w * ITERS + i + 1))
                        pool.tensor_tensor(ebuf[:, h, :, :], ebuf[:, h, :, :],
                                           bn[:, 1:2, :].to_broadcast([P, C, H]), ALU.mult).then_inc(s_mul, 1)
            pool.wait_ge(s_table, 3)
            gather(pool, p_att, n_win, tab_l2)
            ok = counts_hold(pool)
            with pool.If(ok < 1):
                for k in range(3):
                    pool.wait_ge(s_table, 4 + k)
                    gather(pool, p_hop[k], n_win, tab_hop[k])

        @block.scalar
        def _(act):
            act.wait_ge(s_par, 80)
            act.wait_ge(s_set, 4)

            def relu(to, j0, c):
                def work(b, h):
                    for j in range(2):
                        last = S.activation(halves(to, h, 0, H)[j], nb(h, j0 + j)[0:H, 0:HB], ACT.Relu,
                                            bias=col[0:H, c:c + 1])
                    return last
                return work

            def h_to_root(b, h):
                for j in range(2):
                    last = S.activation(blk(feat, H, P, b, j), nb(h, j)[H:P, 0:HB], ACT.Identity,
                                        bias=col[H:P, C_B2:C_B2 + 1])
                return last

            turns(act, d_conv1, [(7, relu(sta, 0, C_BL1)), (9, relu(stb, 2, C_B1)), (11, h_to_root)])
            act.wait_ge(s_dg, 2)
            S.activation(dinv[:, :], dinv2[:, :], ACT.Sqrt).then_inc(s_dg, 1)

            n_win = n_windows(act)
            for u in range(2):
                act.sem_inc(b_st[u], 16)
            act.sem_inc(b_ev, 2)
            side = counts_act(act)
            with act.Fori(0, n_win) as w:
                with act.Fori(0, TITERS) as i:
                    for u in range(2):
                        side(w * TITERS + i, i, u)

            def root_to_sta(b, h):
                return S.copy(sta[H:P, h, :], blk(feat, H, P, b))

            def sta_to_root(b, h):
                return S.copy(blk(feat, H, P, b), sta[H:P, h, :])

            turns(act, d_conv2, [(2, root_to_sta), *ln_act(6), (14, keep_resid), (16, take_feat), (17, sta_to_root)])

            for h in range(2):
                act.sem_inc(s_est[h], 16)
            with act.Fori(0, ITERS) as i:
                for h in range(2):
                    hold(act, s_eh, 2 * i + h + 3)
                    hold(act, s_eacc[1], 2 * i + h + 1)
                    S.activation(emsg[:, h, :, :], ebuf[:, h, :, :], ACT.Square).then_inc(s_esq, 1)
                    act.dma_start(group(edge_h, 2 * i + h), ebuf[:, h, :, :].rearrange("p c f -> p (c f)"))\
                        .then_inc(s_est[h], 16)
            act.wait_ge(s_bn, 5)
            S.activation(bn[:, 2, :], bn[:, 1, :], ACT.Sqrt, bias=eps[:, :]).then_inc(s_bn, 1)
            act.sem_inc(s_msg, 2)
            with act.Fori(0, n_win) as w:
                with act.Fori(0, ITERS) as i:
                    for h in range(2):
                        q = 2 * (w * ITERS + i) + h
                        hold(act, s_mad, q + 1)
                        hold(act, p_msg.summed, q + 1)
                        S.activation(emsg[:, h, :, :], ebuf[:, h, :, :], ACT.Silu).then_inc(s_msg, 1)

            def z_to_feat(b, h):
                for j in range(2):
                    last = S.activation(blk(feat, 0, H, b, j), nb(h, j)[0:H, 0:HB], ACT.Identity,
                                        bias=col[0:H, C_BZ:C_BZ + 1])
                return last

            turns(act, d_z, [(3, z_to_feat)])
            act.wait_ge(s_bnz, 2)
            S.activation(bnz[:, 2:3], bnz[:, 1:2], ACT.Sqrt, bias=eps[0:H, :]).then_inc(s_bnz, 1)
            act.wait_ge(s_bnz, 7)

            def z_silu(b, h):
                return S.activation(sta[0:H, h, :], blk(feat, 0, H, b), ACT.Silu, scale=bnz[:, 2:3], bias=bnz[:, 3:4])

            def keep_hop(b, h):
                return S.copy(tiles(hop, b), nod[:, h, 0, :, :])

            turns(act, d_l1, [(1, z_silu), *ln_act(4), (12, keep_resid), (14, take_feat)])
            act.wait_ge(s_pass, 4)

            def take_hsum(b, h):
                return S.copy(nod[:, h, 1, :, :], tiles(hsum, b))

            ok = counts_hold(act)
            with act.If(ok > 0):
                turns(act, d_l2d, [(1, sums_to_sta), *ln_act(4), (12, keep_resid)])
                act.wait_ge(h_dve[2], H_STEPS[2])
                turns(act, d_out, [(1, take_hsum), (3, take_feat), *ln_act(7)])
            with act.Else():
                turns(act, d_l2, [(1, sums_to_sta), *ln_act(4), (12, keep_resid), (14, keep_hop)])
                for k in range(2):
                    act.wait_ge(s_pass, 5 + k)
                    turns(act, d_hop[k], [(1, sums_to_sta), (5, keep_hop)])
                act.wait_ge(s_pass, 7)
                turns(act, d_hop[2], [(1, sums_to_sta), (6, take_feat), *ln_act(10)])

        @block.tensor
        def _(pe):
            pe.wait_ge(s_lim, 3)
            T.matmul(bank[0][:, 0:P], diag[:, :], ident, start=True, stop=True)
            T.matmul(bank[1][:, 0:P], base_f[:, :], ident, start=True, stop=True).then_inc(s_lim, 1)
            pe.wait_ge(s_lim, 8)
            pe.wait_ge(s_set, 4)
            T.matmul(bank[2][:, 0:P], ones[:, :], diag[:, :], start=True, stop=True)
            T.matmul(bank[3][0:1, 0:P], lim[:, 2:3], ident, start=True, stop=True).then_inc(s_lim, 1)
            pe.wait_ge(s_par, 80)
            n_win = n_windows(pe)

            sum_groups(pe, p_conv1, n_win, lambda h, c: gath[:, h, c, :], gathered(p_conv1), width=P)

            def conv1(b, h):
                for t in range(TB):
                    T.matmul(nb(h, 2)[:, t:t + 1], stb[0:H, h, t * P:(t + 1) * P], ident[0:H, 0:1],
                             start=True, stop=True)
                for j in range(2):
                    last = T.matmul(nb(h, j)[0:H, 0:HB], wts[:, W_CONV1, :], blk(feat, 0, P, b, j),
                                    start=True, stop=True)
                return last

            def mlp1(b, h):
                for j in range(2):
                    last = T.matmul(nb(h, 2 + j)[0:H, 0:HB], wts[0:H, W_MLP1, :], halves(sta, h, 0, H)[j],
                                    start=True, stop=True)
                return last

            def mlp2(b, h):
                for t in range(TB):
                    T.matmul(nb(h, 2)[:, t * H:(t + 1) * H], stb[0:H, h, t * P:(t + 1) * P], wts[0:H, W_MLP2, :],
                             start=True, stop=True)
                for j in range(2):
                    last = T.matmul(nb(h, j)[:, 0:HB], wts[0:H, W_MLP2:W_MLP2 + 2, :].rearrange("p a f -> p (a f)"),
                                    halves(stb, h, 0, H)[j], start=True, stop=True)
                return last

            open_turns(pe, d_conv1)
            pe.wait_ge(s_xf, 16)
            turns(pe, d_conv1, [(5, conv1), (8, mlp1), (10, mlp2)])

            pe.sem_inc(b_mm, 4)
            sum_groups(pe, p_conv2, n_win, lambda h, c: gath[:, h, c, 0:H], gathered(p_conv2), side=counts_pe(pe))

            def conv2(b, h):
                for t in range(TB):
                    last = T.matmul(nb(h, 0)[:, t * H:(t + 1) * H], sta[:, h, t * P:(t + 1) * P], wts[:, W_CONV2, :],
                                    start=True, stop=True)
                return last

            open_turns(pe, d_conv2)
            turns(pe, d_conv2, [(3, conv2), (15, node_by_feat(1)), (18, times_w(W_L1X))])

            with pe.Fori(0, ITERS) as i:
                for h in range(2):
                    hold(pe, s_ef[h], 16 * (i + 1))
                    hold(pe, s_eh, 2 * i + h + 1)
                    for c in range(C):
                        half, at = divmod(c, CA)
                        last = T.matmul(bank[2 * h + half][:, at * H:(at + 1) * H],
                                        eft[half * H:(half + 1) * H, h, at * P:(at + 1) * P],
                                        wts[half * H:(half + 1) * H, W_L1E, :], start=True, stop=True)
                    last.then_inc(s_emm, 1)
            pe.wait_ge(s_eacc[0], GROUPS + 1)
            pe.wait_ge(s_eacc[1], GROUPS + 2)
            for j in range(2):
                for c in range(C):
                    last = T.matmul(bank[4 + j][:, 0:H], ones[:, :], accum[:, j, c, :], start=(c == 0), stop=(c == C - 1))
            last.then_inc(s_bn, 1)
            sum_groups(pe, p_msg, n_win, lambda h, c: emsg[:, h, c, :],
                       lambda pe, k, h: hold(pe, s_msg, 2 * k + h + 3))

            def zlin(b, h):
                for j in range(2):
                    last = T.matmul(nb(h, j)[0:H, 0:HB], wts[:, W_L1Z, :], blk(feat, 0, P, b, j), start=True, stop=True)
                return last

            open_turns(pe, d_z)
            turns(pe, d_z, [(2, zlin)])
            open_turns(pe, d_l1)
            turns(pe, d_l1, [(2, feat_by_node), (13, node_by_feat(1)), (15, times_w(W_L2))])
            pe.wait_ge(s_ok_in, 4)
            T.matmul(bank[2][:, 0:1], ones[:, :], chk[:, 1:2], start=True, stop=True)
            T.matmul(bank[3][0:1, 0:P], chk[:, 0:1], ident, start=True, stop=True).then_inc(s_ok_in, 1)
            sum_groups(pe, p_att, n_win, lambda h, c: gath[:, h, c, 0:H], gathered(p_att))
            ok = counts_hold(pe)
            with pe.If(ok > 0):
                open_turns(pe, d_l2d)
                turns(pe, d_l2d, [(2, feat_by_node)])
                for h in range(2):
                    pe.wait_ge(d_l2d.turn[h], DITERS * d_l2d.steps + 1)
                times_counts(pe, 0, 0)
                pe.wait_ge(h_dve[0], H_STEPS[0])
                times_counts(pe, 1, 1)
                pe.wait_ge(h_dve[1], H_STEPS[1])
                times_counts(pe, 2, 0)
                pe.wait_ge(h_dve[2], H_STEPS[2])
                open_turns(pe, d_out)
                turns(pe, d_out, [(2, node_by_feat(1)), (4, times_w(W_L3))])
            with pe.Else():
                open_turns(pe, d_l2)
                turns(pe, d_l2, [(2, feat_by_node)])
                for k in range(3):
                    sum_groups(pe, p_hop[k], n_win, lambda h, c: gath[:, h, c, 0:H], gathered(p_hop[k]))
                    open_turns(pe, d_hop[k])
                    turns(pe, d_hop[k], [(2, feat_by_node)]
                          + ([(5, node_by_feat(1)), (7, times_w(W_L3))] if k == 2 else []))

        @block.vector
        def _(dve):
            dve.wait_ge(s_dst, 32)
            V.tensor_copy(dst_f[:, :, :].rearrange("p g c -> p (g c)"),
                          wide[:, 0:C * GROUPS].bitcast(i32)).then_inc(s_lim, 1)
            dve.wait_ge(s_lim, 1)
            V.tensor_reduce(diag[:, :], dst_f[:, :, :], AX.X, ALU.min).then_inc(s_lim, 1)
            V.tensor_reduce(base_f[:, :], dst_f[:, :, :], AX.X, ALU.max).then_inc(s_lim, 1)
            dve.wait_ge(s_lim, 4)
            V.tensor_reduce(lim[:, 0:1], bank[0][:, 0:P], AX.X, ALU.min).then_inc(s_lim, 1)
            V.tensor_reduce(lim[:, 1:2], bank[1][:, 0:P], AX.X, ALU.max).then_inc(s_lim, 1)
            dve.wait_ge(s_lim, 6)
            V.tensor_tensor(lim[:, 2:3], lim[:, 1:2], lim[:, 0:1], ALU.subtract).then_inc(s_lim, 1)
            V.tensor_scalar(diag[:, :], ident, lim[:, 0:1], None, ALU.mult).then_inc(s_lim, 1)
            dve.wait_ge(s_lim, 9)
            V.tensor_copy(base_f[:, :], bank[2][:, 0:P]).then_inc(s_lim, 1)
            V.tensor_copy(base_i[:, :], bank[2][0:1, 0:P]).then_inc(s_lim, 1)
            V.tensor_reduce(lim[0:1, 3:4], bank[3][0:1, 0:P], AX.X, ALU.max).then_inc(s_lim, 1)
            dve.wait_ge(s_lim, 12)
            V.tensor_copy(span_i[:, :], lim[0:1, 3:4]).then_inc(s_lim, 1)
            V.tensor_tensor(dst_f[:, :, :], dst_f[:, :, :],
                            base_f[:, :].rearrange("p (g o) -> p g o", o=1).to_broadcast([P, GROUPS, C]),
                            ALU.subtract).then_inc(s_lim, 1)
            dve.wait_ge(s_lim, 14)
            dve.sem_inc(s_win, 1)
            n_win = n_windows(dve)

            dve.wait_ge(s_rec, 32)
            src_w, dst_w = wide[:, WS:WS + FC].bitcast(i32), wide[:, WD:WD + FC].bitcast(i32)
            tmp_w, tmp2_w = wide[:, WT:WT + FC].bitcast(i32), wide[:, WU:WU + FC].bitcast(i32)
            fields = wide[:, WR:WR + 3 * FC].rearrange("p (c r) -> p c r", r=3)
            V.tensor_scalar(tmp_w, src_w, P - 1, None, ALU.bitwise_and).then_inc(s_rec, 1)
            dve.wait_ge(s_rec, 33)
            V.tensor_copy(fields[:, :, 0], tmp_w).then_inc(s_rec, 1)
            V.tensor_scalar(tmp2_w, dst_w, D - 1, None, ALU.bitwise_and).then_inc(s_rec, 1)
            dve.wait_ge(s_rec, 35)
            V.tensor_scalar(tmp_w, src_w, 7, 2, ALU.logical_shift_right, ALU.logical_shift_left).then_inc(s_rec, 1)
            dve.wait_ge(s_rec, 36)
            V.tensor_tensor(fields[:, :, 1], tmp_w, tmp2_w, ALU.add).then_inc(s_rec, 1)
            V.tensor_scalar(dst_w, dst_w, 2, None, ALU.logical_shift_right).then_inc(s_rec, 1)
            dve.wait_ge(s_rec, 38)
            V.tensor_copy(fields[:, :, 2], dst_w).then_inc(s_rec, 1)

            add_windows(dve, p_conv1, n_win, width=P)
            feat_row, wide_row = feat[H:H + 1, 0:NP], wide[H:H + 1, 0:NP]
            dve.wait_ge(s_rec, 55)
            V.tensor_tensor_scan(wide_row, feat_row, feat_row, 0.0, ALU.add, ALU.max).then_inc(s_first, 1)
            V.memset(first_i[:, 0:1], 0).then_inc(s_first, 1)
            dve.wait_ge(s_first, 2)
            V.tensor_copy(first_i[:, 1:BLOCKS], wide_row.rearrange("p (b d) -> p b d", d=D)[:, 0:BLOCKS - 1, D - 1])\
                .then_inc(s_first, 1)

            def take_degree(b, h):
                return V.tensor_copy(stb[0:H, h, :], blk(rdeg, 0, H, b))

            def degree_max(b, h):
                return V.tensor_scalar(blk(rdeg, 0, H, b), blk(rdeg, 0, H, b), 1.0, None, ALU.max)

            def degree_inv(b, h):
                return V.reciprocal(blk(rdeg, 0, H, b), blk(rdeg, 0, H, b))

            def mean(b, h):
                return V.tensor_tensor(blk(feat, 0, H, b), blk(feat, 0, H, b), blk(rdeg, 0, H, b), ALU.mult)

            def degree_by_node(b, h):
                return V.tensor_copy(deg_n[:, bass.ds(b * TB, TB)], nb(h, 2)[:, 0:TB])

            def plus_row(d, j, r):
                def work(b, h):
                    stored(dve, d, b, h)
                    return V.tensor_tensor(nod[:, h, 0, :, :], nodes(h, j), row_b(r), ALU.add)
                return work

            dve.wait_ge(s_deg, 16)
            turns(dve, d_conv1, [(1, take_degree), (2, degree_max), (3, degree_inv), (4, mean), (6, degree_by_node),
                                 (12, plus_row(d_conv1, 2, R_B2))])
            for h in range(2):
                dve.wait_ge(d_conv1.turn[h], DITERS * d_conv1.steps + 1)
            V.tensor_scalar(deg_n[:, :], deg_n[:, :], 1.0, None, ALU.add).then_inc(s_dg, 1)
            dve.wait_ge(s_dg, 1)
            V.reciprocal(dinv2[:, :], deg_n[:, :]).then_inc(s_dg, 1)

            def first_blocks(w=None):
                for u in range(2):
                    last = V.tensor_scalar(blk_w[:, u, :], iota0[:, 0:BT], float(u * BT), None, ALU.add)
                return last

            first_blocks().then_inc(b_tmp, 1)
            dve.sem_inc(b_key, 2)
            dve.sem_inc(b_red, 2)
            V.tensor_copy(ident_b[:, :], ident)

            def again(w):
                hold(dve, b_tmp, 6 * TITERS * (w + 1) + 1)
                first_blocks().then_inc(b_again, 1)
                hold(dve, b_again, w + 1)

            add_windows(dve, p_conv2, n_win, side=counts_dve(dve), after_side=again)
            for u in range(2):
                hold(dve, b_st[u], 16 * TITERS * n_win + 16)

            def mean_to_sta(b, h):
                return V.tensor_tensor(sta[0:H, h, :], blk(feat, 0, H, b), blk(rdeg, 0, H, b), ALU.mult)

            def plus_bias(r):
                def work(b, h):
                    return V.tensor_tensor(nod[:, h, 1, :, :], nod[:, h, 1, :, :], row_b(r), ALU.add)
                return work

            def clear_padding(b, h):
                return V.tensor_tensor(nod[:, h, 0, :, :], nod[:, h, 0, :, :], by_tile(val, b), ALU.mult)

            dve.wait_ge(s_par, 80)
            turns(dve, d_conv2, [(1, mean_to_sta), (4, add_resid), (5, plus_bias(R_BL2)), *ln_dve(6), (13, ln_scale(1)),
                                 (19, plus_row(d_conv2, 3, R_B1)), (20, clear_padding)])

            V.memset(accum[:, :, :, :], 0.0).then_inc(s_eacc[0], 1)
            dve.wait_ge(s_eacc[0], 1)
            dve.sem_inc(s_eacc[1], 2)
            dve.sem_inc(s_eh, 2)
            with dve.Fori(0, ITERS) as i:
                for h in range(2):
                    q = 2 * i + h
                    hold(dve, p_edge.rows_in[h], 16 * C * (i + 1))
                    hold(dve, s_emm, q + 1)
                    hold(dve, s_est[h], 16 * i + 16)
                    for half, (lo, hi) in enumerate(((0, CA), (CA, C))):
                        last = V.tensor_tensor(
                            ebuf[:, h, lo:hi, :], gath[:, h, lo:hi, 0:H],
                            bank[2 * h + half][:, 0:(hi - lo) * H].rearrange("p (c f) -> p c f", f=H), ALU.add)
                    last.then_inc(s_eh, 1)
                    hold(dve, s_eh, q + 3)
                    hold(dve, s_eacc[0], q + 1)
                    V.tensor_tensor(accum[:, 0, :, :], accum[:, 0, :, :], ebuf[:, h, :, :], ALU.add)\
                        .then_inc(s_eacc[0], 1)
                for h in range(2):
                    q = 2 * i + h
                    hold(dve, s_esq, q + 1)
                    hold(dve, s_eacc[1], q + 2)
                    V.tensor_tensor(accum[:, 1, :, :], accum[:, 1, :, :], emsg[:, h, :, :], ALU.add)\
                        .then_inc(s_eacc[1], 1)
            dve.wait_ge(s_bn, 1)
            V.tensor_scalar(bn[:, 0, :], bank[4][:, 0:H], 1.0 / E, None, ALU.mult).then_inc(s_bn, 1)
            V.tensor_scalar(bn[:, 1, :], bank[5][:, 0:H], 1.0 / E, None, ALU.mult).then_inc(s_bn, 1)
            dve.wait_ge(s_bn, 3)
            V.tensor_tensor(bn[:, 2, :], bn[:, 0, :], bn[:, 0, :], ALU.mult).then_inc(s_bn, 1)
            dve.wait_ge(s_bn, 4)
            V.tensor_tensor(bn[:, 1, :], bn[:, 1, :], bn[:, 2, :], ALU.subtract).then_inc(s_bn, 1)
            dve.wait_ge(s_bn, 6)
            V.reciprocal(bn[:, 2, :], bn[:, 2, :]).then_inc(s_bn, 1)
            dve.wait_ge(s_bn, 7)
            V.tensor_tensor(bn[:, 1, :], bn[:, 2, :], row[:, R_G1, :], ALU.mult).then_inc(s_bn, 1)
            dve.wait_ge(s_bn, 8)
            V.tensor_tensor(bn[:, 2, :], bn[:, 0, :], bn[:, 1, :], ALU.mult).then_inc(s_bn, 1)
            dve.wait_ge(s_bn, 9)
            V.tensor_tensor(bn[:, 3, :], row[:, R_BE1, :], bn[:, 2, :], ALU.subtract).then_inc(s_bn, 1)
            dve.wait_ge(s_bn, 10)

            def shift_acts(dve, k, h):
                hold(dve, s_mul, 2 * k + h + 1)
                V.tensor_tensor(ebuf[:, h, :, :], ebuf[:, h, :, :], bn[:, 3:4, :].to_broadcast([P, C, H]), ALU.add)\
                    .then_inc(s_mad, 1)

            add_windows(dve, p_msg, n_win, scale=shift_acts)

            def z_stats(b, h):
                for j in range(2):
                    last = V.bn_stats(stats[:, bass.ds(2 * b + j, 1), :].rearrange("p a s -> p (a s)"),
                                      blk(feat, 0, H, b, j))
                return last

            turns(dve, d_z, [(1, mean), (4, z_stats)])
            for h in range(2):
                dve.wait_ge(d_z.turn[h], DITERS * d_z.steps + 1)
            V.bn_stats(stats[:, 2 * NB - 1, :], feat[0:H, NP - HB:N]).then_inc(s_bnz, 1)
            dve.wait_ge(s_bnz, 1)
            V.bn_aggr(bnz[:, 0:2], stats[:, :, :].rearrange("p a s -> p (a s)")).then_inc(s_bnz, 1)
            dve.wait_ge(s_bnz, 3)
            V.reciprocal(bnz[:, 2:3], bnz[:, 2:3]).then_inc(s_bnz, 1)
            dve.wait_ge(s_bnz, 4)
            V.tensor_tensor(bnz[:, 2:3], bnz[:, 2:3], col[0:H, C_G2:C_G2 + 1], ALU.mult).then_inc(s_bnz, 1)
            dve.wait_ge(s_bnz, 5)
            V.tensor_tensor(bnz[:, 1:2], bnz[:, 0:1], bnz[:, 2:3], ALU.mult).then_inc(s_bnz, 1)
            dve.wait_ge(s_bnz, 6)
            V.tensor_tensor(bnz[:, 3:4], col[0:H, C_BE2:C_BE2 + 1], bnz[:, 1:2], ALU.subtract).then_inc(s_bnz, 1)

            turns(dve, d_l1, [(3, add_resid), *ln_dve(4), (11, ln_scale(1)), (16, plus_row(d_l1, 3, R_HB))])
            hold(dve, b_red, 2 * TITERS * n_win + 2)
            V.tensor_reduce(chk[:, 0:1], caught[:, 0, :], AX.X, ALU.max).then_inc(s_ok_in, 2)
            V.tensor_reduce(chk[:, 1:2], caught[:, 1, :], AX.X, ALU.add).then_inc(s_ok_in, 2)
            dve.wait_ge(s_ok_in, 5)
            V.tensor_reduce(chk[0:1, 2:3], bank[3][0:1, 0:P], AX.X, ALU.max).then_inc(s_ok_in, 1)
            V.tensor_scalar(chk[0:1, 3:4], bank[2][0:1, 0:1], float(E), None, ALU.is_equal).then_inc(s_ok_in, 1)
            dve.wait_ge(s_ok_in, 7)
            V.scalar_tensor_tensor(ok_i[:, :], chk[0:1, 2:3], MAX_COUNT, chk[0:1, 3:4], ALU.is_le, ALU.mult)\
                .then_inc(s_ok_in, 1)
            dve.wait_ge(s_ok_in, 8)
            dve.sem_inc(s_ok, 1)

            dve.wait_ge(s_att, 16)
            add_windows(dve, p_att, n_win, weigh=True)

            def first_hop(b, h):
                stored(dve, d_l2, b, h)
                return V.tensor_tensor(nod[:, h, 0, :, :], nod[:, h, 1, :, :], by_tile(dinv, b), ALU.mult)

            def plus_self(b, h):
                return V.tensor_tensor(nod[:, h, 1, :, :], nodes(h, 0), tiles(hop, b), ALU.add)

            def next_hop(d):
                def work(b, h):
                    stored(dve, d, b, h)
                    return V.tensor_tensor(nod[:, h, 0, :, :], nod[:, h, 1, :, :], by_tile(dinv2, b), ALU.mult)
                return work

            def last_hop(b, h):
                return V.tensor_tensor(nod[:, h, 1, :, :], nod[:, h, 1, :, :], by_tile(dinv, b), ALU.mult)

            def result(b, h):
                stored(dve, d_hop[2], b, h)
                return ln_scale(0)(b, h)

            def scaled(b, h):
                return V.tensor_tensor(nod[:, h, 0, :, :], nod[:, h, 1, :, :], by_tile(dinv, b), ALU.mult)

            def part(a, last=False):
                def work(b, h):
                    return V.tensor_copy(parts[0][:, bass.ds(b * TB, TB), a, :], nod[:, h, 0, :, :])
                return work

            def rest(a):
                def work(b, h):
                    return V.tensor_tensor(nod[:, h, 0, :, :], nod[:, h, 0, :, :],
                                           parts[0][:, bass.ds(b * TB, TB), a, :], ALU.subtract)
                return work

            dve.wait_ge(s_dg, 3)
            ok = counts_hold(dve)
            with dve.If(ok > 0):
                turns(dve, d_l2d, [(3, add_resid), *ln_dve(4), (11, ln_scale(1)), (13, scaled), (14, part(0)),
                                   (15, rest(0)), (16, part(1)), (17, rest(1)), (18, part(2))])
                hop_dve(dve, 0, 1)
                hop_dve(dve, 1, 0)
                hop_dve(dve, 2, None)

                def result_d(b, h):
                    stored(dve, d_out, b, h)
                    return ln_scale(0)(b, h)

                turns(dve, d_out, [(5, lambda b, h: add_resid(b, h, 3)), (6, plus_bias(R_B3)), *ln_dve(7),
                                   (14, result_d)])
            with dve.Else():
                turns(dve, d_l2, [(3, add_resid), *ln_dve(4), (11, ln_scale(1)), (13, first_hop)])
                for k in range(2):
                    add_windows(dve, p_hop[k], n_win)
                    turns(dve, d_hop[k], [(3, plus_self), (4, next_hop(d_hop[k]))])
                add_windows(dve, p_hop[2], n_win)
                turns(dve, d_hop[2], [(3, plus_self), (4, last_hop), (8, lambda b, h: add_resid(b, h, 3)),
                                      (9, plus_bias(R_B3)), *ln_dve(10), (17, result)])


def kernel(**inputs):
    import numpy as _np
    import concourse.bacc as _bacc
    from concourse import mybir as _mybir
    from concourse.bass_utils import run_bass_kernel_spmd as _run

    a = {k: _np.asarray(v) for k, v in inputs.items()}
    f = _np.float32
    ep = GROUPS * C * P
    x_rows = _np.zeros((NP, H), f)
    x_rows[:N] = a["x"]

    def lists(v, fill):
        p = _np.full((ep,), fill, v.dtype)
        p[:E] = v.reshape(E)
        return p.reshape(GROUPS, C, P)

    def flat(v, fill):
        p = _np.full((P * FC,), fill, v.dtype)
        p[:E] = v
        return p.reshape(P, FC)

    edges = _np.zeros((ep, H), f)
    edges[:E] = a["edge_attr_64"]
    edges = edges.reshape(GROUPS, C, P, H)
    edge_feat = _np.zeros((GROUPS, 2, H, CA, P), f)
    edge_feat[:, 0] = edges[:, :CA].transpose(0, 3, 1, 2)
    edge_feat[:, 1, :, :CB] = edges[:, CA:].transpose(0, 3, 1, 2)

    w = _np.zeros((P, 10, H), f)
    w[:H, W_CONV1], w[H:, W_CONV1] = a["L0_gnn_conv1_Wl"].T, a["L0_gnn_conv1_Wr"].T
    w[:H, W_MLP1] = a["L0_gnn_mlp_W1"].T
    w[:H, W_MLP2] = w[:H, W_MLP2 + 1] = a["L0_gnn_mlp_W2"].T
    w[:H, W_CONV2], w[H:, W_CONV2] = a["L0_gnn_conv2_Wl"].T, a["L0_gnn_conv2_Wr"].T
    w[H:, W_L1X] = a["L1_gnn_W1"][:H]
    w[:H, W_L1E] = w[H:, W_L1E] = a["L1_gnn_W1"][H:]
    w[:H, W_L1Z], w[H:, W_L1Z] = a["L1_gnn_W2"][H:], a["L1_gnn_W2"][:H]
    w[H:, W_L2] = a["L2_gnn_weight"]
    w[H:, W_L3] = a["L3_gnn_W"]
    cols = _np.stack([_np.concatenate([a[k], a[k]]) for k in (
        "L0_gnn_conv1_bl", "L0_gnn_mlp_b1", "L0_gnn_mlp_b2", "L1_gnn_b2", "L1_gnn_g2", "L1_gnn_be2")], axis=1)
    rows = _np.stack([a[k] for k in (
        "L0_gnn_mlp_b2", "L0_gnn_conv2_bl", "L1_gnn_b1", "L2_gnn_h_bias", "L3_gnn_b", "L1_gnn_g1", "L1_gnn_be1")])
    rows = _np.broadcast_to(rows, (P,) + rows.shape)
    consts = _np.stack([_np.eye(P, dtype=f), _np.broadcast_to(_np.arange(P, dtype=f), (P, P))], axis=1)
    valid = (_np.arange(NP) < N).astype(f).reshape(NT, P).T

    arrays = dict(
        x_rows=x_rows, x_feat=x_rows.T, src_idx=lists(a["src"], N).transpose(0, 2, 1),
        dst_idx=lists(a["dst"], N).transpose(2, 0, 1).reshape(P, GROUPS * C),
        src_flat=flat(a["src"], 0), dst_flat=flat(a["dst"], NO_NODE), att=lists(a["edge_weight1"], 0).transpose(2, 0, 1), edge_feat=edge_feat.reshape(GROUPS, P, CA * P),
        consts=consts, valid=valid, weights=w, cols=cols, rows=rows)
    nc = _bacc.Bacc("TRN2", target_bir_lowering=False, num_devices=1)
    arrays = {k: _np.ascontiguousarray(v) for k, v in arrays.items()}
    aps = [nc.dram_tensor(k, v.shape, _mybir.dt.from_np(v.dtype), kind="ExternalInput").ap() for k, v in arrays.items()]
    out = nc.dram_tensor("out_rows", (NP, H), _mybir.dt.float32, kind="ExternalOutput").ap()
    gnn_program(nc, *aps, out)
    r = _run(nc, [arrays], core_ids=[0])
    return r.results[0]["out_rows"][:N]
```

```python
import concourse.bass as bass
from concourse import mybir
from contextlib import ExitStack

P = 128
N = 12500
E = 212500
H = 64
NT = -(-N // P)
NP = NT * P
C = 13
GROUPS = -(-E // (P * C))
ITERS = GROUPS // 2
CA = (C + 1) // 2
CB = C - CA
W = 128
TB = 7
NB = NT // TB
BN = TB * P
HB = BN // 2
DITERS = NB // 2
EPS = 1e-5
D = 4
BT = P // D
BLOCKS = NT * BT
FC = -(-(GROUPS * C * P + P) // P // 4) * 4
TITERS = NT // 2
NO_NODE = 1 << 14
PART_SCALE = 4096.0
MAX_COUNT = 16.0
assert GROUPS == P and NB * TB == NT and NB % 2 == 0

W_CONV1, W_MLP1, W_MLP2, W_CONV2, W_L1X, W_L1E, W_L1Z, W_L2, W_L3 = 0, 1, 2, 4, 5, 6, 7, 8, 9
C_BL1, C_B1, C_B2, C_BZ, C_G2, C_BE2 = range(6)
R_B2, R_BL2, R_B1, R_HB, R_B3, R_G1, R_BE1 = range(7)


def gnn_program(nc, x_rows, x_feat, src_idx, dst_idx, src_flat, dst_flat, att, edge_feat, consts, valid, weights,
                cols, rows, out):
    f32, i32 = mybir.dt.float32, mybir.dt.int32
    bf16, f16, f8 = mybir.dt.bfloat16, mybir.dt.float16, mybir.dt.float8e4
    ALU, ACT, AX = mybir.AluOpType, mybir.ActivationFunctionType, mybir.AxisListType
    V, S, T = nc.vector, nc.scalar, nc.tensor
    ctx = ExitStack()
    with ctx:
        def sb(name, shape, dt=f32):
            return ctx.enter_context(nc.sbuf_tensor(name, shape, dt))

        def sem(name):
            return ctx.enter_context(nc.semaphore(name))

        def sems(name, n=2):
            return [sem(f"{name}{i}") for i in range(n)]

        def dram(name, shape):
            return nc.dram_tensor(name, shape, f32, kind="Internal").ap()

        tab_h2, tab_l1, tab_l2 = dram("tab_h2", [NP, H]), dram("tab_l1", [NP, H]), dram("tab_l2", [NP, H])
        tab_hop = [dram(f"tab_hop{k}", [NP, H]) for k in range(3)]
        edge_h = dram("edge_h", [GROUPS, P, C * H])
        record = dram("record", [P * FC, 3])
        first_edge = nc.dram_tensor("first_edge", [1, BLOCKS], i32, kind="Internal").ap()
        counts = nc.dram_tensor("counts", [NT, P, NT * P // 4], f32, kind="Internal").ap()
        degree_row = dram("degree_row", [1, NP])

        feat = sb("feat", [P, NP + W])
        wide = sb("wide", [P, NP])
        rdeg = wide[0:H, :]
        att_s = wide[:, NP - GROUPS * C:NP].rearrange("p (g c) -> p g c", c=C)
        resid = sb("resid", [P, NT, H])
        hop = wide[:, 0:NT * H].rearrange("p (t f) -> p t f", f=H)
        dst_f = sb("dst_f", [P, GROUPS, C])
        idx = sb("idx", [P, 2, C], i32)
        gath = sb("gath", [P, 2, C, 2 * H])
        oneh = sb("oneh", [P, 2, C, W])
        area = sb("area", [P, 2 * BN + 2 * BN + 6 * TB * H + 2 * C * H])
        accum = area[:, 4 * BN + 6 * TB * H:].rearrange("p (s c f) -> p s c f", s=2, f=H)
        cst = sb("cst", [P, 2, P])
        WT, WS, WD, WU, WR = 0, FC, 2 * FC, 3 * FC, 4 * FC
        assert 7 * FC <= NP
        ident, iota0 = cst[:, 0, :], cst[:, 1, :]
        val = sb("val", [P, NT])
        iota_w = sb("iota_w", [P, 1, W])
        ones = sb("ones", [P, P])
        wts = sb("wts", [P, weights.shape[1], H])
        col = sb("col", [P, cols.shape[1]])
        row = sb("row", [P, rows.shape[1], H])
        lim = sb("lim", [P, 4])
        diag = sb("diag", [P, P])
        base_f = sb("base_f", [P, GROUPS])
        base_i = sb("base_i", [1, GROUPS], i32)
        base_w = sb("base_w", [1, GROUPS], i32)
        first_i = oneh[H:H + 1, :, :, :].rearrange("p s c w -> p (s c w)")[:, 0:BLOCKS].bitcast(i32)
        span_i = sb("span_i", [1, 1], i32)
        deg_n = sb("deg_n", [P, NT])
        dinv = sb("dinv", [P, NT])
        dinv2 = sb("dinv2", [P, NT])
        bn = sb("bn", [P, 4, H])
        bnz = sb("bnz", [H, 4])
        stats = sb("stats", [H, 2 * NB, 6])
        sta = area[:, 0:2 * BN].rearrange("p (s n) -> p s n", s=2)
        stb = area[:, 2 * BN:4 * BN].rearrange("p (s n) -> p s n", s=2)
        nod = area[:, 4 * BN:4 * BN + 6 * TB * H].rearrange("p (s a t f) -> p s a t f", s=2, a=3, f=H)
        ln = sb("ln", [P, 2, 3, TB])
        eft = sta
        ebuf = stb[:, :, 0:C * H].rearrange("p s (c f) -> p s c f", f=H)
        emsg = area[:, 4 * BN:4 * BN + 6 * TB * H].rearrange("p (s n) -> p s n", s=2)[:, :, 0:C * H]\
            .rearrange("p s (c f) -> p s c f", f=H)
        TW = NT * P // 4
        slab = [area[:, u * TW:(u + 1) * TW] for u in range(2)]
        pair_oh = area[:, 2 * TW:2 * TW + 8 * NT * D // 2].bitcast(bf16).rearrange("p (b n) -> p b n", b=8)
        low_oh = sb("low_oh", [P, 8, P], bf16)
        rec = sb("rec", [P, 2, BT, 3])
        key = sb("key", [P, 2, BT])
        first_w = sb("first_w", [1, 2, BT], i32)
        blk_w = sb("blk_w", [P, 2, BT])
        wide_iota = sb("wide_iota", [P, NT * D], f16)
        cells = sb("cells", [P, 2, BT // 2])
        caught = sb("caught", [P, 2, NT + 3])
        chk = sb("chk", [P, 4])
        ok_i = sb("ok_i", [1, 1], i32)
        ident_h = sb("ident_h", [P, P], f16)
        tile_in = [t[:, :, :, :].rearrange("p s c w -> p (s c w)")[:, 0:TW] for t in (gath, oneh)]
        parts = [t[:, 0:NT * H].bitcast(f16).rearrange("p (t a f) -> p t a f", a=2, f=H) for t in (wide, feat)]
        hsum = feat[:, 0:NT * H].rearrange("p (t f) -> p t f", f=H)
        eps = sb("eps", [P, 1])

        banks = ctx.enter_context(nc.psum_tensor("banks", [P, 8, 512], f32))
        bank = [banks[:, i, :] for i in range(8)]
        window = [bank[7 * h][:, 0:W] for h in range(2)]

        s_dst, s_par, s_att, s_xf, s_deg = sem("dst_in"), sem("params_in"), sem("att_in"), sem("xfeat_in"), sem("deg_moved")
        s_set = sem("constants_set")
        s_lim = sem("setup_steps")
        s_win = sem("windows_known")
        s_gate = sem("gate")
        s_pre = sem("pass_prepared")
        s_shift = sem("windows_shifted")
        s_pass = sem("pass_done")
        s_table = sem("table_stored")
        s_weighed = sem("onehots_placed")

        def hold(eng, s, value):
            eng.wait_ge(s, value)
            eng.sem_inc(s_gate, 1)

        class Pass:

            def __init__(self, name, gathers=True, sums=True):
                if gathers:
                    self.idx_in = sems(f"{name}_idx_in")
                    self.rows_in = sems(f"{name}_rows_in")
                if not sums:
                    return
                self.onehot = sem(f"{name}_onehot")
                self.summed = sem(f"{name}_summed")
                self.added = sem(f"{name}_added")

        p_conv1, p_conv2, p_att = (Pass(n) for n in ("conv1", "conv2", "att"))
        p_edge, p_msg = Pass("edge", sums=False), Pass("msg", gathers=False)
        p_hop = [Pass(f"hop{k}") for k in range(3)]
        s_ef = sems("edge_feat_in")
        s_emm = sem("edge_product")
        s_eh = sem("edge_act")
        s_esq = sem("edge_squared")
        s_eacc = sems("edge_accumulated")
        s_est = sems("edge_stored")
        s_hl, s_mul = sems("act_loaded"), sem("act_scaled")
        s_mad, s_msg = sem("act_shifted"), sem("message")
        s_rec, s_first, s_fold = sem("records"), sem("first_edges"), sem("residual_steps")
        s_mean, s_zmean = sem("mean_steps"), sem("z_means")
        b_first = sems("b_first_in")
        b_rec = sems("b_records_in")
        b_key = sem("b_keys")
        b_tmp, b_again, b_red = sem("b_steps"), sem("b_again"), sem("b_cells_read")
        b_oh, b_mm, b_ev = sem("b_onehots"), sem("b_products"), sem("b_counts")
        b_st = sems("b_stored")
        s_ok_in, s_ok = sem("counts_check_steps"), sem("counts_checked")
        h_in = [sems(f"h_slot{u}_half_in") for u in range(2)]
        h_mm, h_red, h_dve = sems("h_product", 3), sems("h_summed", 3), sems("h_steps", 3)
        s_bn, s_bnz, s_dg = sem("bn_steps"), sem("bnz_steps"), sem("degree_steps")

        class Turns:

            def __init__(self, name, steps, stores=True):
                self.turn, self.steps = sems(f"{name}_turn"), steps
                if stores:
                    self.stored = sems(f"{name}_stored")

            def wait(self, eng, i, h, step):
                eng.wait_ge(self.turn[h], i * self.steps + step)
                if eng is nc.scalar or eng is nc.gpsimd:
                    eng.sem_inc(s_gate, 1)

        def done(ins, d, h):
            ins.then_inc(d.turn[h], 1)

        d_conv1, d_conv2, d_z, d_l1, d_l2 = (Turns("d_conv1", 7), Turns("d_conv2", 18), Turns("d_z", 3, stores=False),
                                             Turns("d_l1", 15), Turns("d_l2", 13))
        d_l2d, d_out = Turns("d_l2d", 14, stores=False), Turns("d_out", 12)
        d_hop = [Turns("d_hop0", 5), Turns("d_hop1", 5), Turns("d_hop2", 16)]

        block = ctx.enter_context(nc.Block())

        def n_windows(eng):
            eng.wait_ge(s_win, 1)
            return eng.value_load(span_i[0:1, 0:1], min_val=0, max_val=NP) // W + 1

        def group(t, g):
            return t[bass.ds(g, 1), :, :].rearrange("a p c -> (a p) c")

        class Build:

            def __init__(self, first, n, phase):
                self.first, self.n, self.phase = first, n, phase

            def pairs(self, n_win, w):
                return w * self.n if self.phase == 0 else n_win * BUILD_A.n + w * self.n

        BUILD_A, BUILD_B = Build(0, ITERS // 2, 0), Build(ITERS // 2, TITERS - ITERS // 2, 1)

        def steps(side):
            if side is None:
                return [(0, ITERS, 1, None)]
            n = side.build.n
            return [(0, n, 2, side)] + ([(n, ITERS // 2, 2, None)] if n < ITERS // 2 else [])

        def load_lists(sp, p, n_win, used, edge=False, side=None):
            with sp.Fori(0, n_win) as w:
                for lo, hi, body, extra in steps(side):
                    with sp.Fori(lo, hi) as j:
                        for v in range(body):
                            i = body * j + v
                            for h in range(2):
                                if extra is not None and h == 0:
                                    extra.first(j, v)
                                hold(sp, used, 2 * (w * ITERS + i) + h + 1)
                                sp.dma_start(idx[:, h, :], group(src_idx, 2 * i + h)).then_inc(p.idx_in[h], 16)
                                if edge:
                                    sp.dma_start(eft[:, h, :], group(edge_feat, 2 * i + h)).then_inc(s_ef[h], 16)
                                if extra is not None:
                                    extra(w, j, v, h)

        def gather(pool, p, n_win, table):
            with pool.Fori(0, n_win) as w:
                with pool.Fori(0, ITERS) as i:
                    for h in range(2):
                        hold(pool, p.idx_in[h], 16 * (w * ITERS + i + 1))
                        for c in range(C):
                            pool.indirect_dma_start(
                                out=gath[:, h, c, 0:H], out_offset=None, in_=table[:, :],
                                in_offset=bass.IndirectOffsetOnAxis(ap=idx[:, h, c:c + 1], axis=0),
                            ).then_inc(p.rows_in[h], 16)

        def sum_groups(pe, p, n_win, rows_of, rows_are_in, width=H, side=None):
            pe.sem_inc(p.summed, 2)
            with pe.Fori(0, n_win) as w:
                for lo, hi, body, extra in steps(side):
                    with pe.Fori(lo, hi) as j:
                        for v in range(body):
                            i = body * j + v
                            for h in range(2):
                                q = 2 * (w * ITERS + i) + h
                                rows_are_in(pe, w * ITERS + i, h)
                                hold(pe, p.onehot, q + 1)
                                hold(pe, p.added, q + 1)
                                for c in range(C):
                                    last = T.matmul(window[h][0:width, :], rows_of(h, c), oneh[:, h, c, :],
                                                    start=(c == 0), stop=(c == C - 1))
                                last.then_inc(p.summed, 1)
                                if extra is not None:
                                    extra(w, j, v, h)

        def gathered(p):
            return lambda pe, k, h: hold(pe, p.rows_in[h], 16 * C * (k + 1))

        passes = [0]

        def add_windows(dve, p, n_win, width=H, weigh=False, scale=None, side=None):
            V.memset(feat[0:width, :], 0.0).then_inc(s_pre, 1)
            V.tensor_copy(iota_w[:, 0, :], iota0).then_inc(s_pre, 1)
            V.tensor_copy(base_w[:, :], base_i[:, :]).then_inc(s_pre, 1)
            before = passes[0]
            passes[0] += 1
            dve.wait_ge(s_pre, 3 * passes[0])
            dve.sem_inc(p.added, 2)
            with dve.Fori(0, n_win) as w:
                def place(i, h):
                    q = 2 * (w * ITERS + i) + h
                    if scale is not None:
                        scale(dve, w * ITERS + i, h)
                    hold(dve, p.summed, q + 1)
                    ins = V.tensor_tensor(
                        oneh[:, h, :, :], iota_w[:, :, :].to_broadcast([P, C, W]),
                        dst_f[:, bass.ds(2 * i + h, 1), :].rearrange("p a (c o) -> p (a c) o", o=1)
                        .to_broadcast([P, C, W]), ALU.is_equal)
                    if weigh:
                        ins.then_inc(s_weighed, 1)
                        hold(dve, s_weighed, q + 1)
                        ins = V.tensor_tensor(
                            oneh[:, h, :, :], oneh[:, h, :, :],
                            att_s[:, bass.ds(2 * i + h, 1), :].rearrange("p a (c o) -> p (a c) o", o=1)
                            .to_broadcast([P, C, W]), ALU.mult)
                    ins.then_inc(p.onehot, 1)

                def add(i, h):
                    q = 2 * (w * ITERS + i) + h
                    at = base_w[0:1, 2 * i + h:2 * i + h + 1] if isinstance(i, int) \
                        else base_w[0:1, bass.ds(2 * i + h, 1)]
                    first = dve.value_load(at, min_val=0, max_val=NP)
                    hold(dve, p.summed, q + 3)
                    hold(dve, p.added, q + 2)
                    V.tensor_tensor(feat[0:width, bass.ds(first, W)], feat[0:width, bass.ds(first, W)],
                                    window[h][0:width, :], ALU.add).then_inc(p.added, 1)

                def step(j, v, body, extra):
                    i = body * j + v
                    for h in range(2):
                        if not (isinstance(i, int) and i == 0):
                            add(i - 1, h)
                        place(i, h)
                        if extra is None or (isinstance(i, int) and i == h == 0):
                            continue
                        if h == 1:
                            extra(w, j, v, 0)
                        elif v > 0:
                            extra(w, j, v - 1, 1)
                        else:
                            extra(w, j - 1, body - 1, 1)

                for lo, hi, body, extra in steps(side):
                    if lo == 0:
                        for v in range(body):
                            step(0, v, body, extra)
                    with dve.Fori(max(lo, 1), hi) as j:
                        for v in range(body):
                            step(j, v, body, extra)
                    if extra is not None:
                        extra(w, hi - 1, body - 1, 1)
                for h in range(2):
                    add(ITERS - 1, h)
                hold(dve, p.added, 2 * ITERS * (w + 1) + 2)
                V.tensor_scalar(iota_w[:, 0, :], iota_w[:, 0, :], float(W), None, ALU.add).then_inc(s_shift, 1)
                V.tensor_scalar(base_w[:, :], base_w[:, :], float(W), float(NP), ALU.add, ALU.min)\
                    .then_inc(s_shift, 1)
                hold(dve, s_shift, 2 * (n_win * before + w + 1))
                if side is not None:
                    side.after(w)
            dve.sem_inc(s_pass, 1)

        def blk(t, lo, hi, b, half=None):
            if half is None:
                return t[lo:hi, bass.ds(b * BN, BN)]
            return t[lo:hi, bass.ds(b * BN + half * HB, HB)]

        def tiles(t, b):
            return t[:, bass.ds(b * TB, TB), :]

        def by_tile(t, b):
            return t[:, bass.ds(b * TB, TB)].rearrange("p (t o) -> p t o", o=1).to_broadcast([P, TB, H])

        def over_features(t):
            return t.rearrange("p (t o) -> p t o", o=1).to_broadcast([P, TB, H])

        def row_b(r):
            return row[:, r:r + 1, :].to_broadcast([P, TB, H])

        def nb(h, j):
            return bank[4 * h + j]

        def nodes(h, j):
            return nb(h, j)[:, 0:TB * H].rearrange("p (t f) -> p t f", t=TB)

        def halves(t, h, lo, hi):
            return [t[lo:hi, h, j * HB:(j + 1) * HB] for j in range(2)]

        def turns(eng, d, steps):
            lag = d.steps // 2
            even = [(step, 0, 0, step, work) for step, work in steps]
            odd = [(step + lag, 1, 0, step, work) for step, work in steps if step + lag <= d.steps]
            late = [(step + lag - d.steps, 1, 1, step, work) for step, work in steps if step + lag > d.steps]

            def run(i, parts):
                for _, h, back, step, work in sorted(parts, key=lambda part: part[:2]):
                    d.wait(eng, i - back, h, step)
                    done(work(2 * (i - back) + h, h), d, h)

            run(0, even + odd)
            with eng.Fori(1, DITERS) as i:
                run(i, even + odd + late)
            run(DITERS, late)

        def open_turns(pe, d):
            for h in range(2):
                pe.sem_inc(d.turn[h], 1)

        def store(sp, d, table):
            for h in range(2):
                sp.sem_inc(d.stored[h], 16)
            with sp.Fori(0, DITERS) as i:
                for h in range(2):
                    hold(sp, d.turn[h], (i + 1) * d.steps + 1)
                    sp.dma_start(table[bass.ds((2 * i + h) * BN, BN), :].rearrange("(t p) f -> p t f", p=P),
                                 nod[:, h, 0, :, :]).then_inc(d.stored[h], 16)
            for h in range(2):
                sp.wait_ge(d.stored[h], 16 * DITERS + 16)
            sp.sem_inc(s_table, 1)

        def stored(eng, d, i_block, h):
            hold(eng, d.stored[h], 16 * ((i_block - h) // 2) + 16)

        def feat_by_node(b, h):
            for t in range(TB):
                last = T.matmul(nb(h, 0)[:, t * H:(t + 1) * H], sta[0:H, h, t * P:(t + 1) * P], ident[0:H, 0:H],
                                start=True, stop=True)
            return last

        def node_by_feat(src):
            def work(b, h):
                for t in range(TB):
                    j, at = divmod(t, 4)
                    last = T.matmul(nb(h, 1 + j)[H:P, at * P:(at + 1) * P], nod[:, h, src, t, :], ident,
                                    start=True, stop=True)
                return last
            return work

        def take_feat(b, h):
            S.copy(sta[H:P, h, 0:4 * P], nb(h, 1)[H:P, 0:4 * P])
            return S.copy(sta[H:P, h, 4 * P:BN], nb(h, 2)[H:P, 0:3 * P])

        def times_w(w):
            def work(b, h):
                for t in range(TB):
                    last = T.matmul(nb(h, 3)[:, t * H:(t + 1) * H], sta[H:P, h, t * P:(t + 1) * P], wts[H:P, w, :],
                                    start=True, stop=True)
                return last
            return work

        def sums_to_sta(b, h):
            return S.copy(sta[0:H, h, :], blk(feat, 0, H, b))

        def ln_sum(b, h):
            return V.tensor_reduce(ln[:, h, 0, :], nod[:, h, 1, :, :], AX.X, ALU.add)

        def ln_center(b, h):
            return V.scalar_tensor_tensor(nod[:, h, 1, :, :], over_features(ln[:, h, 0, :]), -1.0 / H,
                                          nod[:, h, 1, :, :], ALU.mult, ALU.add)

        def ln_square(b, h):
            return S.activation(nod[:, h, 2, :, :], nod[:, h, 1, :, :], ACT.Square)

        def ln_var(b, h):
            return V.tensor_reduce(ln[:, h, 1, :], nod[:, h, 2, :, :], AX.X, ALU.add)

        def ln_std(b, h):
            return S.activation(ln[:, h, 1, :], ln[:, h, 1, :], ACT.Sqrt, bias=eps[:, :], scale=1.0 / H)

        def ln_rstd(b, h):
            return V.reciprocal(ln[:, h, 1, :], ln[:, h, 1, :])

        def ln_scale(to):
            def work(b, h):
                return V.tensor_tensor(nod[:, h, to, :, :], nod[:, h, 1, :, :], over_features(ln[:, h, 1, :]),
                                       ALU.mult)
            return work

        def keep_resid(b, h):
            return S.copy(tiles(resid, b), nod[:, h, 1, :, :])

        def ln_dve(first):
            return [(first, ln_sum), (first + 1, ln_center), (first + 3, ln_var), (first + 5, ln_rstd)]

        def ln_act(first):
            return [(first + 2, ln_square), (first + 4, ln_std)]

        def add_resid(b, h, j=0):
            return V.tensor_tensor(nod[:, h, 1, :, :], nodes(h, j), tiles(resid, b), ALU.add)

        HALF = BT // 2
        PAIRS = BT // 2

        class Side:

            def __init__(self, build, n_win, work, after=None, ahead=None):
                self.build, self.n_win, self.work, self.after, self.ahead = build, n_win, work, after, ahead

            def first(self, j, u):
                self.ahead(2 * self.build.first + 2 * j + u, u)

            def __call__(self, w, j, u, half):
                self.work(self.build.pairs(self.n_win, w) + j, 2 * self.build.first + 2 * j + u, u, half)

        def counts_sp(sp):
            edge_regs = [sp.alloc_register(f"first_edge{j}") for j in range(16)]

            def ahead(tile, u):
                sp.dma_start(first_w[:, u, :], first_edge[0:1, bass.ds(tile * BT, BT)]).then_inc(b_first[u], 16)

            def work(m, tile, u, half):
                if half == 0:
                    hold(sp, b_key, 2 * m + u + 1)
                    hold(sp, b_first[u], 16 * (m + 1))
                for at in range(half * HALF, (half + 1) * HALF, 16):
                    sp.load(edge_regs, first_w[:, u, at:at + 16])
                    for j in range(16):
                        edge = sp.snap(edge_regs[j], min_val=0, max_val=P * FC - P)
                        sp.dma_start(rec[:, u, at + j, :], record[bass.ds(edge, P), :]).then_inc(b_rec[u], 16)
            return work, ahead

        def counts_dve(dve, build):
            def work(m, tile, u, half):
                if half == 0:
                    hold(dve, b_rec[u], 16 * BT * (m + 1))
                    hold(dve, b_tmp, 6 * m + 3 * u + 1)
                    V.tensor_tensor(key[:, u, :], rec[:, u, :, 2], blk_w[:, u, :], ALU.not_equal).then_inc(b_tmp, 1)
                    hold(dve, b_tmp, 6 * m + 3 * u + 2)
                    V.scalar_tensor_tensor(key[:, u, :], key[:, u, :], float(NT * D), rec[:, u, :, 1], ALU.mult, ALU.add)\
                        .then_inc(b_tmp, 1)
                    hold(dve, b_tmp, 6 * m + 3 * u + 3)
                    V.tensor_scalar(blk_w[:, u, :], blk_w[:, u, :], float(2 * BT), None, ALU.add).then_inc(b_tmp, 1)
                else:
                    hold(dve, b_ev, (2 * m + u) * PAIRS + 2)
                    V.tensor_reduce(caught[:, 0, bass.ds(tile + build.phase, 1)], cells[:, 1 - u, :], AX.X, ALU.max)
                    V.tensor_reduce(caught[:, 1, bass.ds(tile + build.phase, 1)], cells[:, 1 - u, :], AX.X, ALU.add)\
                        .then_inc(b_red, 1)
                for q in range(half * PAIRS // 2, (half + 1) * PAIRS // 2):
                    dve.wait_ge(b_mm, (2 * m + u) * PAIRS + q + 1)
                    for j in range(2):
                        at, ring = 2 * q + j, (2 * q + j) % 8
                        V.tensor_scalar(pair_oh[:, ring, :], wide_iota[:, :], key[:, u, at:at + 1], None, ALU.is_equal)
                        last = V.tensor_scalar(low_oh[:, ring, :], wide_iota[:, 0:P], rec[:, u, at, 0:1], None,
                                               ALU.is_equal)
                    last.then_inc(b_oh, 1)
                if half == 1:
                    hold(dve, b_oh, (2 * m + u + 1) * PAIRS)
                    dve.sem_inc(b_key, 1)
            return work

        def counts_pe(pe):
            def work(m, tile, u, half):
                for q in range(half * PAIRS // 2, (half + 1) * PAIRS // 2):
                    n = (2 * m + u) * PAIRS + q
                    pe.wait_ge(b_oh, n + 1)
                    pe.wait_ge(b_ev, n + 1)
                    for j in range(2):
                        ring = (2 * q + j) % 8
                        last = T.matmul(bank[1 + 2 * (q % 2) + j][:, 0:NT * D], low_oh[:, ring, :],
                                        pair_oh[:, ring, :], start=True, stop=True)
                    last.then_inc(b_mm, 1)
            return work

        def counts_act(act, build, n_win):
            with act.Fori(0, n_win) as w:
                with act.Fori(0, build.n) as j:
                    for u in range(2):
                        m = build.pairs(n_win, w) + j
                        hold(act, b_st[u], 16 * m + 16)
                        hold(act, b_red, 2 * m + u + 1)
                        for q in range(PAIRS):
                            bk = 1 + 2 * (q % 2)
                            hold(act, b_mm, (2 * m + u) * PAIRS + q + 5)
                            to = slab[u].bitcast(f8).rearrange("p (s n) -> p s n", s=NT)[:, :, 2 * D * q:2 * D * (q + 1)]
                            S.activation(to.rearrange("p s (b d) -> p b s d", d=D),
                                         banks[:, bk:bk + 2, 0:NT * D].rearrange("p b (s d) -> p b s d", d=D),
                                         ACT.Copy, saturate=False, accum_out=cells[:, u, q:q + 1]).then_inc(b_ev, 1)
                        hold(act, b_ev, (2 * m + u + 1) * PAIRS + 2)
                        act.dma_start(counts[bass.ds(2 * build.first + 2 * j + u, 1), :, :]
                                      .rearrange("a p n -> (a p) n"), slab[u]).then_inc(b_st[u], 16)

        def counts_in(sp, k):
            with sp.Fori(0, TITERS) as i:
                for u in range(2):
                    for half in range(2):
                        words = slice(half * TW // 2, (half + 1) * TW // 2)
                        hold(sp, h_mm[k], 2 * (2 * i + u) + half + 1)
                        sp.dma_start(tile_in[u][:, words],
                                     counts[bass.ds(2 * i + u, 1), :, words].rearrange("a p n -> (a p) n"))\
                            .then_inc(h_in[u][half], 16)

        def times_counts(pe, k, src):
            with pe.Fori(0, TITERS) as i:
                for u in range(2):
                    hold(pe, h_red[k], 2 * i + u + 1)
                    to = bank[u][:, 0:2 * H]
                    T.matmul(to, ident_h[:, :], parts[src][:, bass.ds(2 * i + u, 1), :, :]
                             .rearrange("p t a f -> p (t a f)"), start=True, stop=False)
                    for half in range(2):
                        hold(pe, h_in[u][half], 16 * (k * TITERS + i + 1))
                        for t in range(half * NT // 2, (half + 1) * NT // 2):
                            last = T.matmul(to, tile_in[u].bitcast(f8)[:, t * P:(t + 1) * P],
                                            parts[src][:, t, :, :].rearrange("p a f -> p (a f)"),
                                            start=False, stop=(t == NT - 1))
                        last.then_inc(h_mm[k], 1)
            if k < 2:
                pe.wait_ge(h_mm[k], 4 * TITERS + 4)
                pe.sem_inc(h_mm[k + 1], 4)

        def hop_dve(dve, k, to):
            dve.sem_inc(h_red[k], 2)
            per = 4 if to is not None else 2
            with dve.Fori(0, TITERS) as i:
                for u in range(2):
                    at = bass.ds(2 * i + u, 1)
                    b = per * (2 * i + u)
                    hold(dve, h_mm[k], 2 * (2 * i + u) + 6)
                    V.tensor_reduce(nod[:, u, 0, 0, :], bank[u][:, 0:2 * H].rearrange("p (a f) -> p f a", a=2),
                                    AX.X, ALU.add).then_inc(h_dve[k], 1)
                    hold(dve, h_dve[k], b + 1)
                    dve.sem_inc(h_red[k], 1)
                    if to is None:
                        V.tensor_scalar(hsum[:, at, :].rearrange("p t f -> p (t f)"), nod[:, u, 0, 0, :], dinv[:, at],
                                        1.0 / PART_SCALE, ALU.mult, ALU.mult).then_inc(h_dve[k], 1)
                        continue
                    V.tensor_scalar(nod[:, u, 1, 0, :], nod[:, u, 0, 0, :], dinv2[:, at], None, ALU.mult)\
                        .then_inc(h_dve[k], 1)
                    hold(dve, h_dve[k], b + 2)

                    def part(a):
                        return parts[to][:, at, a, :].rearrange("p t f -> p (t f)")

                    V.tensor_copy(part(0), nod[:, u, 1, 0, :]).then_inc(h_dve[k], 1)
                    hold(dve, h_dve[k], b + 3)
                    V.tensor_tensor(part(1), nod[:, u, 1, 0, :], part(0), ALU.subtract).then_inc(h_dve[k], 1)

        H_STEPS = [8 * TITERS, 8 * TITERS, 4 * TITERS]

        def counts_hold(eng):
            eng.wait_ge(s_ok, 1)
            return eng.value_load(ok_i[0:1, 0:1], min_val=0, max_val=1)

        @block.sync
        def _(sp):
            sp.dma_start(wide[:, 0:C * GROUPS].bitcast(i32), dst_idx)\
                .then_inc(s_dst, 16)
            sp.dma_start(cst[:, :, :], consts).then_inc(s_dst, 16)
            sp.dma_start(wide[:, WS:WS + FC].bitcast(i32), src_flat).then_inc(s_rec, 16)
            sp.dma_start(wide[:, WD:WD + FC].bitcast(i32), dst_flat).then_inc(s_rec, 16)
            for t, src in ((wts[:, :, :], weights), (col[:, :], cols), (row[:, :, :], rows), (val[:, :], valid),
                           (resid[:, :, :], x_rows.rearrange("(t p) f -> p t f", p=P))):
                sp.dma_start(t, src).then_inc(s_par, 16)
            n_win = n_windows(sp)
            sp.wait_ge(s_rec, 39)
            sp.dma_start(record.rearrange("(p c) r -> p (c r)", p=P), wide[:, WR:WR + 3 * FC]).then_inc(s_rec, 16)

            load_lists(sp, p_conv1, n_win, p_conv1.summed)
            sp.wait_ge(s_pass, 1)
            sp.wait_ge(s_rec, 55)
            sp.dma_start(rdeg[:, :], feat[H:P, 0:NP]).then_inc(s_deg, 16)
            sp.dma_start(wide[H:H + 1, :], feat[H:H + 1, 0:NP]).then_inc(s_deg, 16)
            sp.dma_start(degree_row, feat[H:H + 1, 0:NP]).then_inc(s_deg, 16)
            sp.wait_ge(s_deg, 48)
            sp.dma_start(feat[H:P, 0:NP], x_feat).then_inc(s_xf, 16)
            sp.dma_start(diag[0:NT, :], degree_row.rearrange("o (t p) -> (o t) p", p=P)).then_inc(s_deg, 16)
            sp.wait_ge(s_first, 3)
            sp.dma_start(first_edge, first_i).then_inc(s_first, 16)
            sp.wait_ge(s_first, 19)
            store(sp, d_conv1, tab_h2)
            counts_work, first_edges = counts_sp(sp)
            load_lists(sp, p_conv2, n_win, p_conv2.summed, side=Side(BUILD_A, n_win, counts_work, ahead=first_edges))
            store(sp, d_conv2, tab_l1)

            load_lists(sp, p_edge, 1, s_eh, edge=True)
            for h in range(2):
                sp.wait_ge(s_est[h], 16 * ITERS + 16)
            sp.wait_ge(s_bn, 1)
            with sp.Fori(0, n_win) as w:
                with sp.Fori(0, ITERS) as i:
                    for h in range(2):
                        hold(sp, s_mul, 2 * (w * ITERS + i) + h + 1)
                        sp.dma_start(ebuf[:, h, :, :].rearrange("p c f -> p (c f)"),
                                     group(edge_h, 2 * i + h)).then_inc(s_hl[h], 16)
            store(sp, d_l1, tab_l2)
            sp.dma_start(att_s[:, :, :], att).then_inc(s_att, 16)
            load_lists(sp, p_att, n_win, p_att.summed, side=Side(BUILD_B, n_win, counts_work, ahead=first_edges))
            ok = counts_hold(sp)
            with sp.If(ok > 0):
                for u in range(2):
                    hold(sp, b_st[u], 16 * TITERS * n_win + 16)
                for k in range(3):
                    counts_in(sp, k)
                store(sp, d_out, out)
            with sp.Else():
                store(sp, d_l2, tab_hop[0])
                for k in range(3):
                    load_lists(sp, p_hop[k], n_win, p_hop[k].summed)
                    store(sp, d_hop[k], tab_hop[k + 1] if k < 2 else out)

        @block.gpsimd
        def _(pool):
            pool.memset(gath[:, :, :, :], 1.0).then_inc(s_set, 1)
            pool.memset(ones[:, :], 1.0).then_inc(s_set, 1)
            pool.memset(eps[:, :], EPS).then_inc(s_set, 1)
            pool.iota(wide_iota[:, :], pattern=[[1, NT * D]], base=0, channel_multiplier=0,
                      allow_small_or_imprecise_dtypes=True).then_inc(s_set, 1)
            pool.wait_ge(s_set, 4)
            n_win = n_windows(pool)
            gather(pool, p_conv1, n_win, x_rows)
            pool.wait_ge(s_table, 1)
            gather(pool, p_conv2, n_win, tab_h2)
            pool.wait_ge(s_table, 2)
            gather(pool, p_edge, 1, tab_l1)
            pool.wait_ge(s_bn, 10)
            pool.sem_inc(s_mul, 2)
            with pool.Fori(0, n_win) as w:
                with pool.Fori(0, ITERS) as i:
                    for h in range(2):
                        hold(pool, s_hl[h], 16 * (w * ITERS + i + 1))
                        hold(pool, s_msg, 2 * (w * ITERS + i) + h + 1)
                        pool.tensor_tensor(emsg[:, h, :, :], ebuf[:, h, :, :],
                                           bn[:, 1:2, :].to_broadcast([P, C, H]), ALU.mult).then_inc(s_mul, 1)
            pool.wait_ge(s_table, 3)
            gather(pool, p_att, n_win, tab_l2)
            ok = counts_hold(pool)
            with pool.If(ok < 1):
                for k in range(3):
                    pool.wait_ge(s_table, 4 + k)
                    gather(pool, p_hop[k], n_win, tab_hop[k])

        @block.scalar
        def _(act):
            act.wait_ge(s_par, 80)
            act.wait_ge(s_set, 4)

            def relu(to, j0, c):
                def work(b, h):
                    for j in range(2):
                        last = S.activation(halves(to, h, 0, H)[j], nb(h, j0 + j)[0:H, 0:HB], ACT.Relu,
                                            bias=col[0:H, c:c + 1])
                    return last
                return work

            def h_to_root(b, h):
                for j in range(2):
                    last = S.activation(blk(feat, H, P, b, j), nb(h, j)[H:P, 0:HB], ACT.Identity,
                                        bias=col[H:P, C_B2:C_B2 + 1])
                return last

            turns(act, d_conv1, [(2, relu(sta, 0, C_BL1)), (4, relu(stb, 2, C_B1)), (6, h_to_root)])
            act.wait_ge(s_dg, 3)
            S.activation(dinv[:, :], dinv2[:, :], ACT.Sqrt).then_inc(s_dg, 1)

            n_win = n_windows(act)
            for u in range(2):
                act.sem_inc(b_st[u], 16)
            act.sem_inc(b_ev, 2)
            counts_act(act, BUILD_A, n_win)

            def root_to_sta(b, h):
                return S.copy(sta[H:P, h, :], blk(feat, H, P, b))

            def sta_to_root(b, h):
                return S.copy(blk(feat, H, P, b), sta[H:P, h, :])

            for u in range(2):
                hold(act, b_st[u], 16 * BUILD_A.n * n_win + 16)
            turns(act, d_conv2, [(1, root_to_sta), *ln_act(5), (12, keep_resid), (14, take_feat), (15, sta_to_root)])

            for h in range(2):
                act.sem_inc(s_est[h], 16)
            with act.Fori(0, ITERS) as i:
                for h in range(2):
                    hold(act, s_eh, 2 * i + h + 3)
                    hold(act, s_eacc[1], 2 * i + h + 1)
                    S.activation(emsg[:, h, :, :], ebuf[:, h, :, :], ACT.Square).then_inc(s_esq, 1)
                    act.dma_start(group(edge_h, 2 * i + h), ebuf[:, h, :, :].rearrange("p c f -> p (c f)"))\
                        .then_inc(s_est[h], 16)
            act.wait_ge(s_bn, 5)
            S.activation(bn[:, 2, :], bn[:, 1, :], ACT.Sqrt, bias=eps[:, :]).then_inc(s_bn, 1)
            act.sem_inc(s_msg, 2)
            with act.Fori(0, n_win) as w:
                with act.Fori(0, ITERS) as i:
                    for h in range(2):
                        q = 2 * (w * ITERS + i) + h
                        hold(act, s_mad, q + 1)
                        hold(act, p_msg.summed, q + 1)
                        S.activation(gath[:, h, :, 0:H], emsg[:, h, :, :], ACT.Silu).then_inc(s_msg, 1)

            def z_to_feat(b, h):
                for j in range(2):
                    last = S.activation(blk(feat, 0, H, b, j), nb(h, j)[0:H, 0:HB], ACT.Identity,
                                        bias=col[0:H, C_BZ:C_BZ + 1])
                return last

            turns(act, d_z, [(2, z_to_feat)])
            act.wait_ge(s_bnz, 2)
            S.activation(bnz[:, 2:3], bnz[:, 1:2], ACT.Sqrt, bias=eps[0:H, :]).then_inc(s_bnz, 1)
            act.wait_ge(s_bnz, 7)

            def z_silu(b, h):
                return S.activation(sta[0:H, h, :], blk(feat, 0, H, b), ACT.Silu, scale=bnz[:, 2:3], bias=bnz[:, 3:4])

            def keep_hop(b, h):
                return S.copy(tiles(hop, b), nod[:, h, 0, :, :])

            turns(act, d_l1, [(1, z_silu), *ln_act(4), (11, keep_resid), (13, take_feat)])
            counts_act(act, BUILD_B, n_win)
            for u in range(2):
                hold(act, b_st[u], 16 * TITERS * n_win + 16)
            act.wait_ge(s_pass, 4)

            def take_hsum(b, h):
                return S.copy(nod[:, h, 1, :, :], tiles(hsum, b))

            ok = counts_hold(act)
            with act.If(ok > 0):
                turns(act, d_l2d, [(1, sums_to_sta), *ln_act(4), (11, keep_resid)])
                act.wait_ge(h_dve[2], H_STEPS[2])
                turns(act, d_out, [(1, take_hsum), (3, take_feat), *ln_act(6)])
            with act.Else():
                turns(act, d_l2, [(1, sums_to_sta), *ln_act(4), (11, keep_resid), (13, keep_hop)])
                for k in range(2):
                    act.wait_ge(s_pass, 5 + k)
                    turns(act, d_hop[k], [(1, sums_to_sta), (5, keep_hop)])
                act.wait_ge(s_pass, 7)
                turns(act, d_hop[2], [(1, sums_to_sta), (6, take_feat), *ln_act(10)])

        @block.tensor
        def _(pe):
            pe.wait_ge(s_lim, 3)
            T.matmul(bank[0][:, 0:P], diag[:, :], ident, start=True, stop=True)
            T.matmul(bank[1][:, 0:P], base_f[:, :], ident, start=True, stop=True).then_inc(s_lim, 1)
            pe.wait_ge(s_lim, 8)
            pe.wait_ge(s_set, 4)
            T.matmul(bank[2][:, 0:P], ones[:, :], diag[:, :], start=True, stop=True)
            T.matmul(bank[3][0:1, 0:P], lim[:, 2:3], ident, start=True, stop=True).then_inc(s_lim, 1)
            pe.wait_ge(s_par, 80)
            n_win = n_windows(pe)

            sum_groups(pe, p_conv1, n_win, lambda h, c: gath[:, h, c, :], gathered(p_conv1), width=P)

            def conv1(b, h):
                hold(pe, s_mean, 6 * ((b - h) // 2) + 5 + h)
                for j in range(2):
                    last = T.matmul(nb(h, j)[0:H, 0:HB], wts[:, W_CONV1, :], blk(feat, 0, P, b, j),
                                    start=True, stop=True)
                return last

            def mlp1(b, h):
                pe.sem_inc(s_gate, 1)
                for j in range(2):
                    last = T.matmul(nb(h, 2 + j)[0:H, 0:HB], wts[0:H, W_MLP1, :], halves(sta, h, 0, H)[j],
                                    start=True, stop=True)
                return last

            def mlp2(b, h):
                for t in range(TB):
                    T.matmul(nb(h, 2)[:, t * H:(t + 1) * H], stb[0:H, h, t * P:(t + 1) * P], wts[0:H, W_MLP2, :],
                             start=True, stop=True)
                for j in range(2):
                    last = T.matmul(nb(h, j)[:, 0:HB], wts[0:H, W_MLP2:W_MLP2 + 2, :].rearrange("p a f -> p (a f)"),
                                    halves(stb, h, 0, H)[j], start=True, stop=True)
                return last

            open_turns(pe, d_conv1)
            pe.wait_ge(s_xf, 16)
            turns(pe, d_conv1, [(1, conv1), (3, mlp1), (5, mlp2)])
            pe.wait_ge(s_deg, 64)
            pe.wait_ge(d_conv1.turn[0], DITERS * d_conv1.steps + 1)
            T.matmul(bank[2][:, 0:NT], diag[0:NT, :], ident[0:NT, 0:NT], start=True, stop=True).then_inc(s_dg, 1)

            pe.sem_inc(b_mm, 4)
            sum_groups(pe, p_conv2, n_win, lambda h, c: gath[:, h, c, 0:H], gathered(p_conv2),
                       side=Side(BUILD_A, n_win, counts_pe(pe)))

            def conv2(b, h):
                for t in range(TB):
                    last = T.matmul(nb(h, 0)[:, t * H:(t + 1) * H], sta[:, h, t * P:(t + 1) * P], wts[:, W_CONV2, :],
                                    start=True, stop=True)
                return last

            open_turns(pe, d_conv2)
            turns(pe, d_conv2, [(3, conv2), (12, node_by_feat(1)), (15, times_w(W_L1X))])

            with pe.Fori(0, ITERS) as i:
                for h in range(2):
                    hold(pe, s_ef[h], 16 * (i + 1))
                    hold(pe, s_eh, 2 * i + h + 1)
                    for c in range(C):
                        half, at = divmod(c, CA)
                        last = T.matmul(bank[2 * h + half][:, at * H:(at + 1) * H],
                                        eft[half * H:(half + 1) * H, h, at * P:(at + 1) * P],
                                        wts[half * H:(half + 1) * H, W_L1E, :], start=True, stop=True)
                    last.then_inc(s_emm, 1)
            pe.wait_ge(s_eacc[0], GROUPS + 1)
            pe.wait_ge(s_eacc[1], GROUPS + 2)
            for j in range(2):
                for c in range(C):
                    last = T.matmul(bank[4 + j][:, 0:H], ones[:, :], accum[:, j, c, :], start=(c == 0), stop=(c == C - 1))
            last.then_inc(s_bn, 1)
            sum_groups(pe, p_msg, n_win, lambda h, c: gath[:, h, c, 0:H],
                       lambda pe, k, h: hold(pe, s_msg, 2 * k + h + 3))

            def zlin(b, h):
                hold(pe, s_zmean, b + 1)
                for j in range(2):
                    last = T.matmul(nb(h, j)[0:H, 0:HB], wts[:, W_L1Z, :], blk(feat, 0, P, b, j), start=True, stop=True)
                return last

            open_turns(pe, d_z)
            turns(pe, d_z, [(1, zlin)])
            open_turns(pe, d_l1)
            turns(pe, d_l1, [(2, feat_by_node), (11, node_by_feat(1)), (14, times_w(W_L2))])
            sum_groups(pe, p_att, n_win, lambda h, c: gath[:, h, c, 0:H], gathered(p_att),
                       side=Side(BUILD_B, n_win, counts_pe(pe)))
            pe.wait_ge(s_ok_in, 4)
            T.matmul(bank[2][:, 0:1], ones[:, :], chk[:, 1:2], start=True, stop=True)
            T.matmul(bank[3][0:1, 0:P], chk[:, 0:1], ident, start=True, stop=True).then_inc(s_ok_in, 1)
            ok = counts_hold(pe)
            with pe.If(ok > 0):
                hold(pe, p_att.summed, GROUPS * n_win + 2)
                pe.sem_inc(h_mm[0], 4)
                open_turns(pe, d_l2d)
                turns(pe, d_l2d, [(2, feat_by_node)])
                for h in range(2):
                    pe.wait_ge(d_l2d.turn[h], DITERS * d_l2d.steps + 1)
                times_counts(pe, 0, 0)
                pe.wait_ge(h_dve[0], H_STEPS[0])
                times_counts(pe, 1, 1)
                pe.wait_ge(h_dve[1], H_STEPS[1])
                times_counts(pe, 2, 0)
                pe.wait_ge(h_dve[2], H_STEPS[2])
                open_turns(pe, d_out)
                turns(pe, d_out, [(2, node_by_feat(1)), (4, times_w(W_L3))])
            with pe.Else():
                open_turns(pe, d_l2)
                turns(pe, d_l2, [(2, feat_by_node)])
                for k in range(3):
                    sum_groups(pe, p_hop[k], n_win, lambda h, c: gath[:, h, c, 0:H], gathered(p_hop[k]))
                    open_turns(pe, d_hop[k])
                    turns(pe, d_hop[k], [(2, feat_by_node)]
                          + ([(5, node_by_feat(1)), (7, times_w(W_L3))] if k == 2 else []))

        @block.vector
        def _(dve):
            dve.wait_ge(s_dst, 32)
            V.tensor_copy(dst_f[:, :, :].rearrange("p g c -> p (g c)"),
                          wide[:, 0:C * GROUPS].bitcast(i32)).then_inc(s_lim, 1)
            dve.wait_ge(s_lim, 1)
            V.tensor_reduce(diag[:, :], dst_f[:, :, :], AX.X, ALU.min).then_inc(s_lim, 1)
            V.tensor_reduce(base_f[:, :], dst_f[:, :, :], AX.X, ALU.max).then_inc(s_lim, 1)
            dve.wait_ge(s_lim, 4)
            V.tensor_reduce(lim[:, 0:1], bank[0][:, 0:P], AX.X, ALU.min).then_inc(s_lim, 1)
            V.tensor_reduce(lim[:, 1:2], bank[1][:, 0:P], AX.X, ALU.max).then_inc(s_lim, 1)
            dve.wait_ge(s_lim, 6)
            V.tensor_tensor(lim[:, 2:3], lim[:, 1:2], lim[:, 0:1], ALU.subtract).then_inc(s_lim, 1)
            V.tensor_scalar(diag[:, :], ident, lim[:, 0:1], None, ALU.mult).then_inc(s_lim, 1)
            dve.wait_ge(s_lim, 9)
            V.tensor_copy(base_f[:, :], bank[2][:, 0:P]).then_inc(s_lim, 1)
            V.tensor_copy(base_i[:, :], bank[2][0:1, 0:P]).then_inc(s_lim, 1)
            V.tensor_reduce(lim[0:1, 3:4], bank[3][0:1, 0:P], AX.X, ALU.max).then_inc(s_lim, 1)
            dve.wait_ge(s_lim, 12)
            V.tensor_copy(span_i[:, :], lim[0:1, 3:4]).then_inc(s_lim, 1)
            V.tensor_tensor(dst_f[:, :, :], dst_f[:, :, :],
                            base_f[:, :].rearrange("p (g o) -> p g o", o=1).to_broadcast([P, GROUPS, C]),
                            ALU.subtract).then_inc(s_lim, 1)
            dve.wait_ge(s_lim, 14)
            dve.sem_inc(s_win, 1)
            n_win = n_windows(dve)

            dve.wait_ge(s_rec, 32)
            src_w, dst_w = wide[:, WS:WS + FC].bitcast(i32), wide[:, WD:WD + FC].bitcast(i32)
            tmp_w, tmp2_w = wide[:, WT:WT + FC].bitcast(i32), wide[:, WU:WU + FC].bitcast(i32)
            fields = wide[:, WR:WR + 3 * FC].rearrange("p (c r) -> p c r", r=3)
            V.tensor_scalar(tmp_w, src_w, P - 1, None, ALU.bitwise_and).then_inc(s_rec, 1)
            dve.wait_ge(s_rec, 33)
            V.tensor_copy(fields[:, :, 0], tmp_w).then_inc(s_rec, 1)
            V.tensor_scalar(tmp2_w, dst_w, D - 1, None, ALU.bitwise_and).then_inc(s_rec, 1)
            dve.wait_ge(s_rec, 35)
            V.tensor_scalar(tmp_w, src_w, 7, 2, ALU.logical_shift_right, ALU.logical_shift_left).then_inc(s_rec, 1)
            dve.wait_ge(s_rec, 36)
            V.tensor_tensor(fields[:, :, 1], tmp_w, tmp2_w, ALU.add).then_inc(s_rec, 1)
            V.tensor_scalar(dst_w, dst_w, 2, None, ALU.logical_shift_right).then_inc(s_rec, 1)
            dve.wait_ge(s_rec, 38)
            V.tensor_copy(fields[:, :, 2], dst_w).then_inc(s_rec, 1)

            add_windows(dve, p_conv1, n_win, width=P)
            def mean(b, h):
                return V.tensor_tensor(blk(feat, 0, H, b), blk(feat, 0, H, b), blk(rdeg, 0, H, b), ALU.mult)

            def means(i):
                for h in range(2):
                    rd = blk(rdeg, 0, H, 2 * i + h)
                    V.tensor_scalar(rd, rd, 1.0, None, ALU.max).then_inc(s_mean, 1)
                for h in range(2):
                    rd = blk(rdeg, 0, H, 2 * i + h)
                    hold(dve, s_mean, 6 * i + 1 + h)
                    V.reciprocal(rd, rd).then_inc(s_mean, 1)
                for h in range(2):
                    hold(dve, s_mean, 6 * i + 3 + h)
                    mean(2 * i + h, h).then_inc(s_mean, 1)

            def plus_row(d, j, r):
                def work(b, h):
                    stored(dve, d, b, h)
                    return V.tensor_tensor(nod[:, h, 0, :, :], nodes(h, j), row_b(r), ALU.add)
                return work

            def fold_bias(r):
                V.tensor_tensor(resid[:, :, :], resid[:, :, :], row[:, r:r + 1, :].to_broadcast([P, NT, H]), ALU.add)\
                    .then_inc(s_fold, 1)

            dve.wait_ge(s_deg, 48)
            means(0)
            wide_row = wide[H:H + 1, 0:NP]
            dve.wait_ge(s_rec, 55)
            V.tensor_tensor_scan(wide_row, wide_row, wide_row, 0.0, ALU.add, ALU.max).then_inc(s_first, 1)
            V.memset(first_i[:, 0:1], 0).then_inc(s_first, 1)
            dve.wait_ge(s_first, 2)
            V.tensor_copy(first_i[:, 1:BLOCKS], wide_row.rearrange("p (b d) -> p b d", d=D)[:, 0:BLOCKS - 1, D - 1])\
                .then_inc(s_first, 1)
            h_rows = plus_row(d_conv1, 2, R_B2)

            def rows_of_blocks(i):
                for h in range(2):
                    d_conv1.wait(dve, i, h, 7)
                    done(h_rows(2 * i + h, h), d_conv1, h)

            with dve.Fori(0, DITERS - 1) as i:
                means(i + 1)
                rows_of_blocks(i)
            rows_of_blocks(DITERS - 1)
            dve.wait_ge(s_par, 80)
            fold_bias(R_BL2)
            dve.wait_ge(s_dg, 1)
            V.tensor_scalar(deg_n[:, :], bank[2][:, 0:NT], 1.0, None, ALU.add).then_inc(s_dg, 1)
            dve.wait_ge(s_dg, 2)
            V.reciprocal(dinv2[:, :], deg_n[:, :]).then_inc(s_dg, 1)

            def counts_side(build):
                tile0, k0 = 2 * build.first, build.phase

                def prepare():
                    for u in range(2):
                        V.tensor_scalar(blk_w[:, u, :], iota0[:, 0:BT], float((tile0 + u) * BT), None, ALU.add)
                    return V.memset(cells[:, 1, :], 0.0)

                def after(w):
                    pairs = build.pairs(n_win, w + 1)
                    hold(dve, b_tmp, 6 * pairs + 1)
                    hold(dve, b_ev, 2 * pairs * PAIRS + 2)
                    hold(dve, b_red, 2 * pairs + 1)
                    end = tile0 + 2 * build.n + k0
                    V.tensor_reduce(caught[:, 0, end:end + 1], cells[:, 1, :], AX.X, ALU.max)
                    V.tensor_reduce(caught[:, 1, end:end + 1], cells[:, 1, :], AX.X, ALU.add).then_inc(b_again, 1)
                    hold(dve, b_again, 2 * (w + k0 * n_win) + 1)
                    prepare().then_inc(b_again, 1)
                    hold(dve, b_again, 2 * (w + k0 * n_win) + 2)

                return prepare, Side(build, n_win, counts_dve(dve, build), after)

            prepare, side = counts_side(BUILD_A)
            V.memset(caught[:, :, :], 0.0)
            prepare().then_inc(b_tmp, 1)
            dve.sem_inc(b_key, 2)
            dve.sem_inc(b_red, 1)
            V.tensor_copy(ident_h[:, :], ident)
            dve.wait_ge(s_first, 19)
            add_windows(dve, p_conv2, n_win, side=side)
            for u in range(2):
                hold(dve, b_st[u], 16 * BUILD_A.n * n_win + 16)

            def mean_to_sta(b, h):
                return V.tensor_tensor(sta[0:H, h, :], blk(feat, 0, H, b), blk(rdeg, 0, H, b), ALU.mult)

            def plus_bias(r):
                def work(b, h):
                    return V.tensor_tensor(nod[:, h, 1, :, :], nod[:, h, 1, :, :], row_b(r), ALU.add)
                return work

            def clear_padding(b, h):
                return V.tensor_tensor(nod[:, h, 0, :, :], nod[:, h, 0, :, :], by_tile(val, b), ALU.mult)

            dve.wait_ge(s_fold, 1)
            turns(dve, d_conv2, [(1, mean_to_sta), (4, add_resid), *ln_dve(5), (11, ln_scale(1)),
                                 (17, plus_row(d_conv2, 3, R_B1)), (18, clear_padding)])

            V.memset(accum[:, :, :, :], 0.0).then_inc(s_eacc[0], 1)
            dve.wait_ge(s_eacc[0], 1)
            dve.sem_inc(s_eacc[1], 2)
            dve.sem_inc(s_eh, 2)
            with dve.Fori(0, ITERS) as i:
                for h in range(2):
                    q = 2 * i + h
                    hold(dve, p_edge.rows_in[h], 16 * C * (i + 1))
                    hold(dve, s_emm, q + 1)
                    hold(dve, s_est[h], 16 * i + 16)
                    for half, (lo, hi) in enumerate(((0, CA), (CA, C))):
                        last = V.tensor_tensor(
                            ebuf[:, h, lo:hi, :], gath[:, h, lo:hi, 0:H],
                            bank[2 * h + half][:, 0:(hi - lo) * H].rearrange("p (c f) -> p c f", f=H), ALU.add)
                    last.then_inc(s_eh, 1)
                    hold(dve, s_eh, q + 3)
                    hold(dve, s_eacc[0], q + 1)
                    V.tensor_tensor(accum[:, 0, :, :], accum[:, 0, :, :], ebuf[:, h, :, :], ALU.add)\
                        .then_inc(s_eacc[0], 1)
                for h in range(2):
                    q = 2 * i + h
                    hold(dve, s_esq, q + 1)
                    hold(dve, s_eacc[1], q + 2)
                    V.tensor_tensor(accum[:, 1, :, :], accum[:, 1, :, :], emsg[:, h, :, :], ALU.add)\
                        .then_inc(s_eacc[1], 1)
            dve.wait_ge(s_bn, 1)
            V.tensor_scalar(bn[:, 0, :], bank[4][:, 0:H], 1.0 / E, None, ALU.mult).then_inc(s_bn, 1)
            V.tensor_scalar(bn[:, 1, :], bank[5][:, 0:H], 1.0 / E, None, ALU.mult).then_inc(s_bn, 1)
            dve.wait_ge(s_bn, 3)
            V.tensor_tensor(bn[:, 2, :], bn[:, 0, :], bn[:, 0, :], ALU.mult).then_inc(s_bn, 1)
            dve.wait_ge(s_bn, 4)
            V.tensor_tensor(bn[:, 1, :], bn[:, 1, :], bn[:, 2, :], ALU.subtract).then_inc(s_bn, 1)
            dve.wait_ge(s_bn, 6)
            V.reciprocal(bn[:, 2, :], bn[:, 2, :]).then_inc(s_bn, 1)
            dve.wait_ge(s_bn, 7)
            V.tensor_tensor(bn[:, 1, :], bn[:, 2, :], row[:, R_G1, :], ALU.mult).then_inc(s_bn, 1)
            dve.wait_ge(s_bn, 8)
            V.tensor_tensor(bn[:, 2, :], bn[:, 0, :], bn[:, 1, :], ALU.mult).then_inc(s_bn, 1)
            dve.wait_ge(s_bn, 9)
            V.tensor_tensor(bn[:, 3, :], row[:, R_BE1, :], bn[:, 2, :], ALU.subtract).then_inc(s_bn, 1)
            dve.wait_ge(s_bn, 10)

            def shift_acts(dve, k, h):
                hold(dve, s_mul, 2 * k + h + 3)
                V.tensor_tensor(emsg[:, h, :, :], emsg[:, h, :, :], bn[:, 3:4, :].to_broadcast([P, C, H]), ALU.add)\
                    .then_inc(s_mad, 1)

            add_windows(dve, p_msg, n_win, scale=shift_acts)

            def z_stats(b, h):
                for j in range(2):
                    last = V.bn_stats(stats[:, bass.ds(2 * b + j, 1), :].rearrange("p a s -> p (a s)"),
                                      blk(feat, 0, H, b, j))
                return last

            def z_means(i):
                for h in range(2):
                    mean(2 * i + h, h).then_inc(s_zmean, 1)

            def z_stats_of_blocks(i):
                for h in range(2):
                    d_z.wait(dve, i, h, 3)
                    done(z_stats(2 * i + h, h), d_z, h)

            z_means(0)
            with dve.Fori(0, DITERS - 1) as i:
                z_means(i + 1)
                z_stats_of_blocks(i)
            z_stats_of_blocks(DITERS - 1)
            for h in range(2):
                dve.wait_ge(d_z.turn[h], DITERS * d_z.steps + 1)
            V.bn_stats(stats[:, 2 * NB - 1, :], feat[0:H, NP - HB:N]).then_inc(s_bnz, 1)
            dve.wait_ge(s_bnz, 1)
            V.bn_aggr(bnz[:, 0:2], stats[:, :, :].rearrange("p a s -> p (a s)")).then_inc(s_bnz, 1)
            dve.wait_ge(s_bnz, 3)
            V.reciprocal(bnz[:, 2:3], bnz[:, 2:3]).then_inc(s_bnz, 1)
            dve.wait_ge(s_bnz, 4)
            V.tensor_tensor(bnz[:, 2:3], bnz[:, 2:3], col[0:H, C_G2:C_G2 + 1], ALU.mult).then_inc(s_bnz, 1)
            dve.wait_ge(s_bnz, 5)
            V.tensor_tensor(bnz[:, 1:2], bnz[:, 0:1], bnz[:, 2:3], ALU.mult).then_inc(s_bnz, 1)
            dve.wait_ge(s_bnz, 6)
            V.tensor_tensor(bnz[:, 3:4], col[0:H, C_BE2:C_BE2 + 1], bnz[:, 1:2], ALU.subtract).then_inc(s_bnz, 1)

            turns(dve, d_l1, [(3, add_resid), *ln_dve(4), (10, ln_scale(1)), (15, plus_row(d_l1, 3, R_HB))])
            dve.wait_ge(s_att, 16)
            prepare, side = counts_side(BUILD_B)
            prepare().then_inc(s_fold, 1)
            dve.wait_ge(s_fold, 2)
            add_windows(dve, p_att, n_win, weigh=True, side=side)
            V.tensor_reduce(chk[:, 0:1], caught[:, 0, :], AX.X, ALU.max).then_inc(s_ok_in, 2)
            V.tensor_reduce(chk[:, 1:2], caught[:, 1, :], AX.X, ALU.add).then_inc(s_ok_in, 2)
            dve.wait_ge(s_ok_in, 5)
            V.tensor_reduce(chk[0:1, 2:3], bank[3][0:1, 0:P], AX.X, ALU.max).then_inc(s_ok_in, 1)
            V.tensor_scalar(chk[0:1, 3:4], bank[2][0:1, 0:1], float(E), None, ALU.is_equal).then_inc(s_ok_in, 1)
            dve.wait_ge(s_ok_in, 7)
            V.scalar_tensor_tensor(ok_i[:, :], chk[0:1, 2:3], MAX_COUNT, chk[0:1, 3:4], ALU.is_le, ALU.mult)\
                .then_inc(s_ok_in, 1)
            dve.wait_ge(s_ok_in, 8)
            dve.sem_inc(s_ok, 1)

            def first_hop(b, h):
                stored(dve, d_l2, b, h)
                return V.tensor_tensor(nod[:, h, 0, :, :], nod[:, h, 1, :, :], by_tile(dinv, b), ALU.mult)

            def plus_self(b, h):
                return V.tensor_tensor(nod[:, h, 1, :, :], nodes(h, 0), tiles(hop, b), ALU.add)

            def next_hop(d):
                def work(b, h):
                    stored(dve, d, b, h)
                    return V.tensor_tensor(nod[:, h, 0, :, :], nod[:, h, 1, :, :], by_tile(dinv2, b), ALU.mult)
                return work

            def last_hop(b, h):
                return V.tensor_tensor(nod[:, h, 1, :, :], nod[:, h, 1, :, :], by_tile(dinv, b), ALU.mult)

            def result(b, h):
                stored(dve, d_hop[2], b, h)
                return ln_scale(0)(b, h)

            def scaled(b, h):
                return V.scalar_tensor_tensor(nod[:, h, 0, :, :], nod[:, h, 1, :, :], PART_SCALE, by_tile(dinv, b),
                                              ALU.mult, ALU.mult)

            def high(b, h):
                return V.tensor_copy(parts[0][:, bass.ds(b * TB, TB), 0, :], nod[:, h, 0, :, :])

            def low(b, h):
                return V.tensor_tensor(parts[0][:, bass.ds(b * TB, TB), 1, :], nod[:, h, 0, :, :],
                                       parts[0][:, bass.ds(b * TB, TB), 0, :], ALU.subtract)

            dve.wait_ge(s_dg, 4)
            ok = counts_hold(dve)
            with dve.If(ok > 0):
                turns(dve, d_l2d, [(3, add_resid), *ln_dve(4), (10, ln_scale(1)), (11, scaled), (13, high),
                                   (14, low)])
                for h in range(2):
                    dve.wait_ge(d_l2d.turn[h], DITERS * d_l2d.steps + 1)
                fold_bias(R_B3)
                dve.wait_ge(s_fold, 3)
                hop_dve(dve, 0, 1)
                hop_dve(dve, 1, 0)
                hop_dve(dve, 2, None)

                def result_d(b, h):
                    stored(dve, d_out, b, h)
                    return ln_scale(0)(b, h)

                turns(dve, d_out, [(5, lambda b, h: add_resid(b, h, 3)), *ln_dve(6), (12, result_d)])
            with dve.Else():
                turns(dve, d_l2, [(3, add_resid), *ln_dve(4), (10, ln_scale(1)), (12, first_hop)])
                for k in range(2):
                    add_windows(dve, p_hop[k], n_win)
                    turns(dve, d_hop[k], [(3, plus_self), (4, next_hop(d_hop[k]))])
                add_windows(dve, p_hop[2], n_win)
                turns(dve, d_hop[2], [(3, plus_self), (4, last_hop), (8, lambda b, h: add_resid(b, h, 3)),
                                      (9, plus_bias(R_B3)), *ln_dve(10), (16, result)])


def kernel(**inputs):
    import numpy as _np
    import concourse.bacc as _bacc
    from concourse import mybir as _mybir
    from concourse.bass_utils import run_bass_kernel_spmd as _run

    a = {k: _np.asarray(v) for k, v in inputs.items()}
    f = _np.float32
    ep = GROUPS * C * P
    x_rows = _np.zeros((NP, H), f)
    x_rows[:N] = a["x"]

    def lists(v, fill):
        p = _np.full((ep,), fill, v.dtype)
        p[:E] = v.reshape(E)
        return p.reshape(GROUPS, C, P)

    def flat(v, fill):
        p = _np.full((P * FC,), fill, v.dtype)
        p[:E] = v
        return p.reshape(P, FC)

    edges = _np.zeros((ep, H), f)
    edges[:E] = a["edge_attr_64"]
    edges = edges.reshape(GROUPS, C, P, H)
    edge_feat = _np.zeros((GROUPS, 2, H, CA, P), f)
    edge_feat[:, 0] = edges[:, :CA].transpose(0, 3, 1, 2)
    edge_feat[:, 1, :, :CB] = edges[:, CA:].transpose(0, 3, 1, 2)

    w = _np.zeros((P, 10, H), f)
    w[:H, W_CONV1], w[H:, W_CONV1] = a["L0_gnn_conv1_Wl"].T, a["L0_gnn_conv1_Wr"].T
    w[:H, W_MLP1] = a["L0_gnn_mlp_W1"].T
    w[:H, W_MLP2] = w[:H, W_MLP2 + 1] = a["L0_gnn_mlp_W2"].T
    w[:H, W_CONV2], w[H:, W_CONV2] = a["L0_gnn_conv2_Wl"].T, a["L0_gnn_conv2_Wr"].T
    w[H:, W_L1X] = a["L1_gnn_W1"][:H]
    w[:H, W_L1E] = w[H:, W_L1E] = a["L1_gnn_W1"][H:]
    w[:H, W_L1Z], w[H:, W_L1Z] = a["L1_gnn_W2"][H:], a["L1_gnn_W2"][:H]
    w[H:, W_L2] = a["L2_gnn_weight"]
    w[H:, W_L3] = a["L3_gnn_W"]
    cols = _np.stack([_np.concatenate([a[k], a[k]]) for k in (
        "L0_gnn_conv1_bl", "L0_gnn_mlp_b1", "L0_gnn_mlp_b2", "L1_gnn_b2", "L1_gnn_g2", "L1_gnn_be2")], axis=1)
    rows = _np.stack([a[k] for k in (
        "L0_gnn_mlp_b2", "L0_gnn_conv2_bl", "L1_gnn_b1", "L2_gnn_h_bias", "L3_gnn_b", "L1_gnn_g1", "L1_gnn_be1")])
    rows = _np.broadcast_to(rows, (P,) + rows.shape)
    consts = _np.stack([_np.eye(P, dtype=f), _np.broadcast_to(_np.arange(P, dtype=f), (P, P))], axis=1)
    valid = (_np.arange(NP) < N).astype(f).reshape(NT, P).T

    arrays = dict(
        x_rows=x_rows, x_feat=x_rows.T, src_idx=lists(a["src"], N).transpose(0, 2, 1),
        dst_idx=lists(a["dst"], N).transpose(2, 0, 1).reshape(P, GROUPS * C),
        src_flat=flat(a["src"], 0), dst_flat=flat(a["dst"], NO_NODE), att=lists(a["edge_weight1"], 0).transpose(2, 0, 1), edge_feat=edge_feat.reshape(GROUPS, P, CA * P),
        consts=consts, valid=valid, weights=w, cols=cols, rows=rows)
    nc = _bacc.Bacc("TRN2", target_bir_lowering=False, num_devices=1)
    arrays = {k: _np.ascontiguousarray(v) for k, v in arrays.items()}
    aps = [nc.dram_tensor(k, v.shape, _mybir.dt.from_np(v.dtype), kind="ExternalInput").ap() for k, v in arrays.items()]
    out = nc.dram_tensor("out_rows", (NP, H), _mybir.dt.float32, kind="ExternalOutput").ap()
    gnn_program(nc, *aps, out)
    r = _run(nc, [arrays], core_ids=[0])
    return r.results[0]["out_rows"][:N]
```
